# Optimizing a Trainium2 kernel written in Bass

```python
import numpy as np
import jax
import jax.numpy as jnp

def _softmax(x, axis=-1):
    return jax.nn.softmax(x, axis=axis)

def _gelu(x):
    return jax.nn.gelu(x, approximate=True)

def _silu(x):
    return jax.nn.silu(x)

def _sigmoid(x):
    return jax.nn.sigmoid(x)

def _layernorm(x, axis=-1, eps=1e-05):
    m = jnp.mean(x, axis=axis, keepdims=True)
    v = jnp.var(x, axis=axis, keepdims=True)
    return (x - m) / jnp.sqrt(v + eps)

def _scatter_add(tgt, idx, src, axis=0):
    return tgt.at[idx].add(src)

def _segment_sum(src, seg, n):
    return jax.ops.segment_sum(src, seg, n)
kernel_name = 'mk_hybrid_d1_jaxref_r4_ee3ffe'

def setup_inputs(seed: int=0):
    np.random.seed(seed)
    _w = jnp.asarray

    def _L0_attn_a_setup():
        import jax, jax.numpy as jnp
        import numpy as np
        B, T, C, H = (2, 512, 256, 16)
        key = jax.random.key(seed)
        ks = jax.random.split(key, 6)
        x = jax.random.normal(ks[0], (B, T, C), dtype=jnp.float32)
        wq = jax.random.normal(ks[1], (C, H * 3), dtype=jnp.float32) * C ** (-0.5)
        wk = jax.random.normal(ks[2], (C, H * 3), dtype=jnp.float32) * C ** (-0.5)
        wv = jax.random.normal(ks[3], (C, C), dtype=jnp.float32) * C ** (-0.5)
        wo = jax.random.normal(ks[4], (C, C), dtype=jnp.float32) * C ** (-0.5)
        dirs = jax.random.normal(ks[5], (H, 3), dtype=jnp.float32)
        head_dirs = dirs / jnp.linalg.norm(dirs, axis=1, keepdims=True)
        scale = jnp.full((1,), 1.0 / np.sqrt(3.0), dtype=jnp.float32)
        return {'x': x, 'wq': wq, 'wk': wk, 'wv': wv, 'wo': wo, 'head_dirs': head_dirs, 'scale': scale}
    _L0_attn_a_in = _L0_attn_a_setup()

    def _L0_attn_b_setup():
        import jax, jax.numpy as jnp
        import numpy as np
        ALPHA = 1.2
        A = 1.0
        BANDWIDTH = 1.0
        D_INTRINSIC = 2
        SPHERE_RADIUS = 1.0
        NUM_HEADS = 16
        HIDDEN = 256
        HEAD_DIM = HIDDEN // NUM_HEADS
        EPS = 1e-07

        def _l2norm(t):
            n = jnp.sqrt(jnp.sum(t * t, axis=-1, keepdims=True))
            return t / jnp.maximum(n, 1e-12)
        key = jax.random.key(seed)
        k1, k2, k3, k4, k5 = jax.random.split(key, 5)
        B, S = (2, 512)
        scale = 0.02
        return {'x': jax.random.normal(k1, (B, S, HIDDEN), dtype=jnp.float32), 'w_qkv': jax.random.normal(k2, (3 * HIDDEN, HIDDEN), dtype=jnp.float32) * scale, 'b_qkv': jnp.zeros((3 * HIDDEN,), dtype=jnp.float32), 'w_out': jax.random.normal(k3, (HIDDEN, HIDDEN), dtype=jnp.float32) * scale, 'b_out': jnp.zeros((HIDDEN,), dtype=jnp.float32)}
    _L0_attn_b_in = _L0_attn_b_setup()

    def _L0_ffn_setup():
        import jax, jax.numpy as jnp
        import numpy as np
        B, S, H, E = (4, 512, 256, 8)
        key = jax.random.key(seed)
        k1, k2, k3 = jax.random.split(key, 3)
        scale_w = 1.0 / np.sqrt(H)
        return {'x': jax.random.normal(k1, (B, S, H), dtype=jnp.float32), 'router_w': jax.random.normal(k2, (H, E), dtype=jnp.float32) * scale_w, 'router_b': jnp.zeros((E,), dtype=jnp.float32), 'expert_w': jax.random.normal(k3, (E, H, H), dtype=jnp.float32) * scale_w, 'expert_b': jnp.zeros((E, H), dtype=jnp.float32)}
    _L0_ffn_in = _L0_ffn_setup()
    _d = {'L0_attn_a_x': _L0_attn_a_in['x'], 'L0_attn_a_wq': _L0_attn_a_in['wq'], 'L0_attn_a_wk': _L0_attn_a_in['wk'], 'L0_attn_a_wv': _L0_attn_a_in['wv'], 'L0_attn_a_wo': _L0_attn_a_in['wo'], 'L0_attn_a_head_dirs': _L0_attn_a_in['head_dirs'], 'L0_attn_a_scale': _L0_attn_a_in['scale'], 'L0_attn_b_w_qkv': _L0_attn_b_in['w_qkv'], 'L0_attn_b_b_qkv': _L0_attn_b_in['b_qkv'], 'L0_attn_b_w_out': _L0_attn_b_in['w_out'], 'L0_attn_b_b_out': _L0_attn_b_in['b_out'], 'L0_ffn_router_w': _L0_ffn_in['router_w'], 'L0_ffn_router_b': _L0_ffn_in['router_b'], 'L0_ffn_expert_w': _L0_ffn_in['expert_w'], 'L0_ffn_expert_b': _L0_ffn_in['expert_b']}
    _x0 = _d['L0_attn_a_x']
    _d['L0_attn_a_x'] = jax.random.normal(jax.random.fold_in(jax.random.key(seed), 1), (2, 2048, 256), dtype=_x0.dtype)
    del _x0
    return _d

def reference(L0_attn_a_x, L0_attn_a_wq, L0_attn_a_wk, L0_attn_a_wv, L0_attn_a_wo, L0_attn_a_head_dirs, L0_attn_a_scale, L0_attn_b_w_qkv, L0_attn_b_b_qkv, L0_attn_b_w_out, L0_attn_b_b_out, L0_ffn_router_w, L0_ffn_router_b, L0_ffn_expert_w, L0_ffn_expert_b):

    def _L0_attn_a_ref(x, wq, wk, wv, wo, head_dirs, scale):
        import jax, jax.numpy as jnp
        import numpy as np
        B, T, C, H = (2, 512, 256, 16)
        b, t, c = x.shape
        h = head_dirs.shape[0]
        hd = c // h
        q3 = (x @ wq).reshape(b, t, h, 3).transpose(0, 2, 1, 3)
        k3 = (x @ wk).reshape(b, t, h, 3).transpose(0, 2, 1, 3)
        v = (x @ wv).reshape(b, t, h, hd).transpose(0, 2, 1, 3)
        q_on_dir = jnp.einsum('bhtd,hd->bht', q3, head_dirs)
        k_on_dir = jnp.einsum('bhtd,hd->bht', k3, head_dirs)
        dot_scores = jnp.einsum('bhtd,bhsd->bhts', q3, k3) * scale
        geo_bias = q_on_dir[..., :, None] * k_on_dir[..., None, :]
        scores = dot_scores + geo_bias
        causal = jnp.tril(jnp.ones((t, t), dtype=bool))
        scores = jnp.where(causal, scores, -jnp.inf)
        attn = jax.nn.softmax(scores, axis=-1)
        out = jnp.einsum('bhts,bhsd->bhtd', attn, v)
        out = out.transpose(0, 2, 1, 3).reshape(b, t, c)
        return out @ wo

    def _L0_attn_b_ref(x, w_qkv, b_qkv, w_out, b_out):
        import jax, jax.numpy as jnp
        import numpy as np
        ALPHA = 1.2
        A = 1.0
        BANDWIDTH = 1.0
        D_INTRINSIC = 2
        SPHERE_RADIUS = 1.0
        NUM_HEADS = 16
        HIDDEN = 256
        HEAD_DIM = HIDDEN // NUM_HEADS
        EPS = 1e-07

        def _l2norm(t):
            n = jnp.sqrt(jnp.sum(t * t, axis=-1, keepdims=True))
            return t / jnp.maximum(n, 1e-12)
        B, S, H = x.shape
        qkv = x @ w_qkv.T + b_qkv
        q, k, v = jnp.split(qkv, 3, axis=-1)
        to_heads = lambda t: t.reshape(B, S, NUM_HEADS, HEAD_DIM).transpose(0, 2, 1, 3)
        q = _l2norm(to_heads(q))
        k = _l2norm(to_heads(k))
        v = to_heads(v)
        cos = jnp.einsum('bhsd,bhtd->bhst', q, k)
        g_dist = jnp.arccos(jnp.clip(cos, -1.0 + EPS, 1.0 - EPS)) * SPHERE_RADIUS
        attn_score = (1.0 + g_dist / BANDWIDTH ** 0.5) ** (-D_INTRINSIC - ALPHA)
        n_r = jnp.sum(attn_score, axis=-1)
        n_c = jnp.sum(attn_score, axis=-2)
        k_tilde = (n_r ** (-A))[..., :, None] * attn_score * (n_c ** (-A))[..., None, :]
        probs = k_tilde / jnp.maximum(jnp.sum(k_tilde, axis=-1, keepdims=True), 1e-12)
        out = jnp.einsum('bhst,bhtd->bhsd', probs, v)
        out = out.transpose(0, 2, 1, 3).reshape(B, S, H)
        return out @ w_out.T + b_out

    def _L0_ffn_ref(x, router_w, router_b, expert_w, expert_b):
        import jax, jax.numpy as jnp
        import numpy as np
        B, S, H, E = (4, 512, 256, 8)
        b, s, h = x.shape
        xt = x.reshape(b * s, h)
        logits = xt @ router_w + router_b
        probs = jax.nn.softmax(logits, axis=-1)
        gate = jnp.max(probs, axis=-1)
        idx = jnp.argmax(probs, axis=-1)
        out_all = jnp.einsum('th,ehd->ted', xt, expert_w) + expert_b[None, :, :]
        e_out = jnp.take_along_axis(out_all, idx[:, None, None], axis=1)[:, 0, :]
        y = gate[:, None] * e_out
        return y.reshape(b, s, h)
    x = L0_attn_a_x
    x = x + _L0_attn_a_ref(_layernorm(x, axis=-1), L0_attn_a_wq, L0_attn_a_wk, L0_attn_a_wv, L0_attn_a_wo, L0_attn_a_head_dirs, L0_attn_a_scale)
    x = x + _L0_ffn_ref(_layernorm(x, axis=-1), L0_ffn_router_w, L0_ffn_router_b, L0_ffn_expert_w, L0_ffn_expert_b)
    x = x + _L0_attn_b_ref(_layernorm(x, axis=-1), L0_attn_b_w_qkv, L0_attn_b_b_qkv, L0_attn_b_w_out, L0_attn_b_b_out)
    x = x + _L0_ffn_ref(_layernorm(x, axis=-1), L0_ffn_router_w, L0_ffn_router_b, L0_ffn_expert_w, L0_ffn_expert_b)
    return x

_drawn_inputs = setup_inputs


def setup_inputs(seed=0):
    import zlib

    import numpy as np

    out = dict(_drawn_inputs(seed))
    spreads = {'L0_attn_b_b_qkv': (0.0, 0.1),
     'L0_attn_b_b_out': (0.0, 0.1),
     'L0_ffn_router_b': (0.0, 0.1),
     'L0_ffn_expert_b': (0.0, 0.1)}
    factors = {'L0_attn_b_w_qkv': 3.267}
    for name, (base, spread) in spreads.items():
        noise = np.random.default_rng([zlib.crc32(name.encode()), seed]).standard_normal(out[name].shape)
        drawn = base * np.exp(spread * noise) if base else spread * noise
        out[name] = jnp.asarray(drawn.astype(out[name].dtype))
    for name, factor in factors.items():
        out[name] = (out[name] * factor).astype(out[name].dtype)
    return out
```

```python
from contextlib import ExitStack

import numpy as np

import concourse.bass as bass
from concourse import mybir

F32 = mybir.dt.float32
BF16 = mybir.dt.bfloat16
ALU = mybir.AluOpType
ACT = mybir.ActivationFunctionType
AX = mybir.AxisListType.X
ds = bass.ds

P = 128
B, T, C, H = 2, 2048, 256, 16
HD = C // H
KC = C // P
NT = T // P
CH = 4
NCH = NT // CH
NTT = B * NT
CW = CH * P
NE = 8
BH = B * H
CHUNK_STEPS = 3
LN_EPS = 1e-5
MASKED = -1e30
BANK = 512

A_TERMS = [(0, 0), (0, 1), (0, 2), (1, 0), (1, 1), (2, 0)]
A_D = 4
A_ROWS = A_D * len(A_TERMS)
A_K = A_ROWS + 3
B_QRUNS = [(0, 3), (1, 3), (2, 2)]
B_KRUNS = [(0, 3), (0, 3), (0, 2)]
CLIP = 1.0 - 1e-7
POWER = -3.2
PAIRS = NT // 2
AHEAD = 5
PSC = 3
DVE_SQUARES = ()
ONE8, TWO8 = 0x38, 0x40


class Linked:

    def __init__(self, eng, sem, base=0):
        self.eng, self.sem, self.base, self.n = eng, sem, base, 0

    def __call__(self, ins):
        self.n += 1
        ins.then_inc(self.sem, 1)
        self.eng.wait_ge(self.sem, self.base + self.n)


def hybrid_kernel(nc, io, last_stage=99):
    with ExitStack() as whole:
        def sb(name, shape, dt=F32, ctx=whole):
            return ctx.enter_context(nc.sbuf_tensor(name, shape, dt))

        def ps(name, shape, dt=F32, ctx=whole):
            return ctx.enter_context(nc.psum_tensor(name, shape, dt))

        VO = sb("VO", [P, BH, NT, HD])
        MEAN = sb("MEAN", [P, NTT])
        RS = sb("RS", [P, NTT])
        identf = sb("identf", [P, P])
        x_place = ExitStack()

        def place_x(name):
            return sb(name, [P, NTT, C], ctx=x_place)

        X = place_x("X")
        VO_tiles = VO[:].rearrange("p (b h) t d -> p b h t d", b=B)
        parts_a = {s: nc.dram_tensor(f"parts_a_{s}", [BH, len(A_TERMS), A_D, T], BF16).ap() for s in "qk"}
        parts_b = {s: nc.dram_tensor(f"parts_b_{s}", [BH, 3, HD, T], BF16).ap() for s in "qk"}

        x_kept = nc.dram_tensor("x_kept", [B, T, C], F32).ap()

        def stats_scratch(name, ctx):
            return (sb(name + "_moments", [P, CH, 6], ctx=ctx), sb(name + "_meanvar", [P, CH, 2], ctx=ctx),
                    sb(name + "_gate_word", [P, 1], ctx=ctx))

        def chunk_stats(link, n, scratch):
            moments, meanvar, word = scratch
            nc.vector.memset(word[:], 0.0)
            for t in range(CH):
                last = nc.vector.bn_stats(moments[:, t, :], X[:, ds(n * CH + t, 1), :].rearrange("p a n -> p (a n)"))
            link(last)
            nc.vector.memset(word[:], 0.0)
            for t in range(CH):
                last = nc.vector.bn_aggr(meanvar[:, t, :], moments[:, t, :])
            link(last)
            nc.vector.tensor_scalar(MEAN[:, ds(n * CH, CH)], meanvar[:, :, 0], 1.0, None, ALU.mult)
            link(nc.vector.tensor_scalar(RS[:, ds(n * CH, CH)], meanvar[:, :, 1], LN_EPS, None, ALU.add))

        def normalise_tile(out, tile):
            return nc.vector.tensor_scalar(out, X[:, ds(tile, 1), :].rearrange("p a n -> p (a n)"),
                                           MEAN[:, ds(tile, 1)], RS[:, ds(tile, 1)], ALU.subtract, ALU.mult)

        def rstd_stage(name):
            with ExitStack() as ctx:
                rooted = ctx.enter_context(nc.semaphore(name + "_rooted"))
                with nc.Block() as block:
                    @block.scalar
                    def _(act):
                        nc.scalar.activation(RS[:], RS[:], ACT.Sqrt).then_inc(rooted, 1)

                    @block.vector
                    def _(dve):
                        dve.wait_ge(rooted, 1)
                        nc.vector.reciprocal(RS[:], RS[:])

        def load_stage():
            with ExitStack() as ctx:
                st = stats_scratch("ld", ctx)
                x_in = ctx.enter_context(nc.semaphore("x_in"))
                consts_in = ctx.enter_context(nc.semaphore("consts_in"))
                steps = ctx.enter_context(nc.semaphore("ld_steps"))
                with nc.Block() as block:
                    @block.sync
                    def _(sp):
                        for b in range(B):
                            sp.dma_start(X[:, b * NT:(b + 1) * NT, :],
                                         io["x"][b].rearrange("(t p) c -> p t c", p=P)).then_inc(x_in, 16)
                        sp.dma_start(identf[:], io["ident"]).then_inc(consts_in, 16)
                        sp.wait_ge(consts_in, 16)

                    @block.vector
                    def _(dve):
                        dve.wait_ge(x_in, 16 * B)
                        with dve.Fori(0, B * NCH) as c:
                            chunk_stats(Linked(dve, steps, c * CHUNK_STEPS), c, st)

        def project_a_stage():
            with ExitStack() as ctx:
                def sem(name):
                    return ctx.enter_context(nc.semaphore("pa_" + name))

                wqk = sb("pa_wqk", [P, KC, 112], ctx=ctx)
                wv = sb("pa_wv", [P, KC, C], ctx=ctx)
                spread = sb("pa_spread", [112, P], ctx=ctx)
                qscale = sb("pa_qscale", [P, 1], ctx=ctx)
                xn = sb("pa_xn", [P, CH, C], ctx=ctx)
                xnT = sb("pa_xnT", [P, KC, CW], ctx=ctx)
                qk3 = sb("pa_qk3", [112, CW], ctx=ctx)
                z = sb("pa_z", [P, CW], ctx=ctx)
                rest = sb("pa_rest", [P, CW], ctx=ctx)
                part = [sb(f"pa_part{i}", [P, CW], BF16, ctx=ctx) for i in range(3)]
                psT = ps("pa_psT", [P, KC, CW], ctx=ctx)
                psV = ps("pa_psV", [P, CH, C], ctx=ctx)
                psQ = ps("pa_psQ", [P, CW], ctx=ctx)
                psZ = ps("pa_psZ", [P, CW], ctx=ctx)
                weights_in, normed, transposed, xnT_ready = sem("weights_in"), sem("normed"), sem("transposed"), sem("xnT_ready")
                v_ready, v_taken, q_ready, q_taken = sem("v_ready"), sem("v_taken"), sem("q_ready"), sem("q_taken")
                z_ready, z_taken, split, stored = sem("z_ready"), sem("z_taken"), sem("split"), sem("stored")
                with nc.Block() as block:
                    @block.sync
                    def _(sp):
                        sp.dma_start(wqk[:], io["wqk"].rearrange("(k p) n -> p k n", p=P)).then_inc(weights_in, 16)
                        sp.dma_start(wv[:], io["wv"].rearrange("(k p) n -> p k n", p=P)).then_inc(weights_in, 16)
                        sp.dma_start(spread[:], io["spread"]).then_inc(weights_in, 16)
                        sp.dma_start(qscale[:], io["qscale"]).then_inc(weights_in, 16)
                        n_store = 2 * len(A_TERMS)
                        with sp.Fori(0, B) as b:
                            with sp.Fori(0, NCH) as c:
                                sp.wait_ge(split, (b * NCH + c) * 3 + 3)
                                for s, half in (("q", 0), ("k", 1)):
                                    for j, terms in enumerate(A_TERMS):
                                        src = part[terms[half]][64 * half:64 * half + 64, :]
                                        dst = parts_a[s][ds(b * H, H), j, :, ds(c * CW, CW)]
                                        sp.dma_start(dst, src).then_inc(stored, 16)
                        sp.wait_ge(stored, B * NCH * n_store * 16)

                    @block.vector
                    def _(dve):
                        with dve.Fori(0, B) as b:
                            with dve.Fori(0, NCH) as c:
                                n = b * NCH + c
                                dve.wait_ge(transposed, n)
                                for t in range(CH):
                                    normalise_tile(xn[:, t, :], n * CH + t).then_inc(normed, 1)
                                dve.wait_ge(q_ready, n + 1)
                                nc.vector.tensor_copy(qk3[:], psQ[0:112, :]).then_inc(q_taken, 1)
                                dve.wait_ge(v_ready, n + 1)
                                for t in range(CH):
                                    dst = VO_tiles[:, ds(b, 1), :, ds(c * CH + t, 1), :].rearrange("p a h t d -> p (a h) (t d)")
                                    nc.vector.tensor_copy(dst, psV[:, t, :].rearrange("p (h d) -> p h d", h=H)).then_inc(v_taken, 1)
                                dve.wait_ge(z_taken, n * 3 + 2)
                                nc.vector.tensor_tensor(rest[:], z[:], part[0][:], ALU.subtract).then_inc(split, 1)
                                dve.wait_ge(z_taken, n * 3 + 3)
                                nc.vector.tensor_tensor(part[2][:], rest[:], part[1][:], ALU.subtract).then_inc(split, 2)

                    @block.scalar
                    def _(act):
                        act.wait_ge(weights_in, 64)
                        with act.Fori(0, B * NCH) as n:
                            act.wait_ge(transposed, n + 1)
                            act.wait_ge(v_ready, n)
                            nc.scalar.activation(xnT[:], psT[:], ACT.Copy).then_inc(xnT_ready, 1)
                            act.wait_ge(z_ready, n + 1)
                            act.wait_ge(stored, n * (2 * len(A_TERMS) * 16))
                            nc.scalar.activation(z[:], psZ[:], ACT.Copy, scale=qscale[:]).then_inc(z_taken, 1)
                            act.wait_ge(z_taken, n * 3 + 1)
                            nc.scalar.activation(part[0][:], z[:], ACT.Copy).then_inc(z_taken, 1)
                            act.wait_ge(split, n * 3 + 1)
                            nc.scalar.activation(part[1][:], rest[:], ACT.Copy).then_inc(z_taken, 1)

                    @block.tensor
                    def _(pe):
                        pe.wait_ge(weights_in, 64)
                        with pe.Fori(0, B * NCH) as n:
                            pe.wait_ge(xnT_ready, n)
                            for t in range(CH):
                                pe.wait_ge(normed, n * CH + t + 1)
                                for k in range(KC):
                                    last = nc.tensor.transpose(psT[:, k, t * P:(t + 1) * P], xn[:, t, k * P:(k + 1) * P], identf[:])
                            last.then_inc(transposed, 1)
                            pe.wait_ge(xnT_ready, n + 1)
                            pe.wait_ge(q_taken, n)
                            for k in range(KC):
                                last = nc.tensor.matmul(psQ[0:112, :], wqk[:, k, :], xnT[:, k, :], start=(k == 0), stop=(k == KC - 1))
                            last.then_inc(q_ready, 1)
                            pe.wait_ge(v_taken, n * CH)
                            for t in range(CH):
                                for k in range(KC):
                                    last = nc.tensor.matmul(psV[:, t, :], xnT[:, k, t * P:(t + 1) * P], wv[:, k, :],
                                                            start=(k == 0), stop=(k == KC - 1))
                            last.then_inc(v_ready, 1)
                            pe.wait_ge(q_taken, n + 1)
                            pe.wait_ge(z_taken, n * 3)
                            nc.tensor.matmul(psZ[:], spread[:], qk3[:], start=True, stop=True).then_inc(z_ready, 1)

        def head_out(head):
            return VO[:, ds(head, 1), :, :].rearrange("p a (m j) d -> p (a m) j d", j=CH)

        def times_values(acc, strip, values, weights, first_tile, stop):
            m0 = max(0, -(-(first_tile - strip) // CH))
            if m0 >= CH:
                return None
            moving = weights.rearrange("p (m j n) -> p m j n", j=CH, n=P)[:, m0:, strip, :]
            return nc.tensor.matmul(acc[32 * strip:32 * strip + 32, m0 * P:BANK], values, moving,
                                    start=stop[0], stop=stop[1], skip_group_check=True)

        def attention_a_stage():
            units1 = [(i, c, min(c + BANK, (i + 1) * P)) for i in range(NT) for c in range(0, (i + 1) * P, BANK)]
            units2 = [(i, max(i * P, c), c + 2 * BANK) for i in range(NT) for c in range(0, T, 2 * BANK) if c + 2 * BANK > i * P]
            n1, n2 = len(units1), len(units2)
            pt_bufs = 4
            with ExitStack() as ctx:
                def sem(name):
                    return ctx.enter_context(nc.semaphore("aa_" + name))

                q1 = [sb(f"aa_q1_{i}", [P, T], BF16, ctx=ctx) for i in range(2)]
                k1 = [sb(f"aa_k1_{i}", [P, T], BF16, ctx=ctx) for i in range(2)]
                q2 = [sb(f"aa_q2_{i}", [P, T], BF16, ctx=ctx) for i in range(2)]
                k2 = [sb(f"aa_k2_{i}", [P, T], BF16, ctx=ctx) for i in range(2)]
                pt = [sb(f"aa_pt{i}", [P, T], ctx=ctx) for i in range(pt_bufs)]
                vst = [sb(f"aa_vst{i}", [P, NT, 32], ctx=ctx) for i in range(2)]
                masks = sb("aa_masks", [P, 2, P], ctx=ctx)
                maskb = sb("aa_maskb", [P, 2, P], BF16, ctx=ctx)
                identb = sb("aa_identb", [P, P], BF16, ctx=ctx)
                pmax = sb("aa_pmax", [P, CH, NT], ctx=ctx)
                negmax = sb("aa_negmax", [P, NT], ctx=ctx)
                mrest = sb("aa_mrest", [P, NT], ctx=ctx)
                mparts = sb("aa_mparts", [P, P], BF16, ctx=ctx)
                zeros = sb("aa_zeros", [P, NT], ctx=ctx)
                word = sb("aa_word", [P, 1], ctx=ctx)
                mrow = sb("aa_mrow", [3 * NT, P], BF16, ctx=ctx)
                u = sb("aa_u", [P, BANK], ctx=ctx)
                rsum = sb("aa_rsum", [P, CH, CH], ctx=ctx)
                ps1 = [ps(f"aa_ps1_{i}", [P, BANK], ctx=ctx) for i in range(2)]
                ps2 = [ps(f"aa_ps2_{i}", [P, 2 * BANK], ctx=ctx) for i in range(2)]
                acc = ps("aa_acc", [P, BANK], ctx=ctx)
                psT = ps("aa_psT", [P, CH, P], ctx=ctx)
                psM = psT[:, 0, :].bitcast(BF16)[:, 0:P]
                u_view = psT[:].rearrange("p m (j e) -> p m j e", j=CH)
                masks_in, cleared, consts = sem("masks_in"), sem("cleared"), sem("consts")
                in1, in2 = [sem("in1_0"), sem("in1_1")], [sem("in2_0"), sem("in2_1")]
                ready1, taken1 = sem("ready1"), sem("taken1")
                ready2, exped = sem("ready2"), sem("exped")
                pv_done = sem("pv_done")
                split = sem("split")
                m_turned, m_row, m_in = sem("m_turned"), sem("m_row"), sem("m_in")
                v_copied, acc_copied = sem("v_copied"), sem("acc_copied")
                u_turned, normalised = sem("u_turned"), sem("normalised")
                summed, max_steps, clear_steps = sem("summed"), sem("max_steps"), sem("clear_steps")
                max_links, split_links = CH, 5

                def all_steps(eng, step):
                    step(0, 0, 0)
                    step(1, 1, 0)
                    with eng.Fori(1, BH // 2 - 1) as k:
                        step(k * 2, 0, k)
                        step(k * 2 + 1, 1, k)
                    step(BH - 2, 0, BH // 2 - 1)
                    step(BH - 1, 1, BH // 2 - 1)

                def at_first(s):
                    return isinstance(s, int) and s == 0

                def has_head(s, n):
                    return not isinstance(s, int) or s + n < BH

                with nc.Block() as block:
                    @block.sync
                    def _(sp):
                        sp.dma_start(masks[:], io["masks"].rearrange("m p n -> p m n")).then_inc(masks_in, 16)
                        sp.wait_ge(cleared, 1)

                        def load(head, q, k, done):
                            for side, dst in (("q", q), ("k", k)):
                                src = parts_a[side][ds(head, 1)].rearrange("a e r t -> (a e r) t")
                                sp.dma_start(dst[0:A_ROWS, :], src).then_inc(done, 16)

                        def load_max(head, par):
                            sp.wait_ge(m_row, head + 1)
                            sp.dma_start(q2[par][A_ROWS:A_K, :].rearrange("a (t n) -> a t n", n=P), mrow[:]).then_inc(m_in, 16)

                        for g in range(2):
                            load(g, q1[g], k1[g], in1[g])
                            load(g, q2[g], k2[g], in2[g])
                        load_max(0, 0)
                        for g in range(2):
                            sp.wait_ge(ready1, n1 * (g + 1))
                            load(g + 2, q1[g], k1[g], in1[g])

                        def step(s, par, half):
                            if has_head(s, 1):
                                load_max(s + 1, 1 - par)
                            if has_head(s, 4):
                                sp.wait_ge(ready1, n1 * (s + 3))
                                load(s + 4, q1[par], k1[par], in1[par])
                            if has_head(s, 2):
                                sp.wait_ge(ready2, n2 * (s + 1))
                                load(s + 2, q2[par], k2[par], in2[par])

                        with sp.Fori(0, BH // 2 - 2) as k:
                            step(k * 2, 0, k)
                            step(k * 2 + 1, 1, k)
                        for s in range(BH - 4, BH):
                            step(s, s % 2, s // 2)

                    @block.vector
                    def _(dve):
                        link = Linked(dve, clear_steps)
                        for stack in q1 + k1 + q2:
                            nc.vector.memset(stack[:].bitcast(mybir.dt.uint32), 0)
                        for stack in k2:
                            link(nc.vector.memset(stack[:].bitcast(mybir.dt.uint32), 0))
                            nc.vector.memset(stack[0:A_K, :], 1.0)
                        for v in vst:
                            link(nc.vector.memset(v[:], 0.0))
                            nc.vector.memset(v[:, :, HD], 1.0)
                        nc.vector.memset(mparts[:].bitcast(mybir.dt.uint32), 0)
                        nc.vector.memset(zeros[:], 0.0)
                        nc.vector.memset(rsum[:], 0.0).then_inc(cleared, 1)
                        dve.wait_ge(masks_in, 16)
                        nc.vector.tensor_copy(maskb[:], masks[:])
                        nc.vector.tensor_copy(identb[:], identf[:]).then_inc(consts, 1)

                        def normalise(head):
                            dve.wait_ge(u_turned, head + 1)
                            nc.vector.reciprocal(rsum[:], u_view[:, :, :, HD]).then_inc(summed, 1)
                            dve.wait_ge(summed, head + 1)
                            nc.vector.tensor_tensor(head_out(head), u_view[:, :, :, 0:HD],
                                                    rsum[:].unsqueeze(3).broadcast_to([P, CH, CH, HD]),
                                                    ALU.mult).then_inc(normalised, 1)

                        def maxima(head, before=None):
                            for n, (i, c0, c1) in enumerate(units1):
                                dve.wait_ge(ready1, head * n1 + (n + 1))
                                nc.vector.tensor_reduce(pmax[:, c0 // BANK, i:i + 1], ps1[n % 2][:, 0:c1 - c0], AX,
                                                        ALU.max).then_inc(taken1, 1)
                                if n == 6 and before is not None:
                                    normalise(before)
                            dve.wait_ge(taken1, head * n1 + n1)
                            steps = Linked(dve, max_steps, head * max_links)
                            for c in range(1, CH):
                                steps(nc.vector.tensor_tensor(pmax[:, 0, CH * c:], pmax[:, 0, CH * c:], pmax[:, c, CH * c:], ALU.max))
                            dve.wait_ge(split, head * split_links)
                            steps(nc.vector.tensor_scalar(negmax[:], pmax[:, 0, :], -1.0, None, ALU.mult))

                        maxima(0)
                        maxima(1)

                        def step(s, par, half):
                            before = None if at_first(s) else s - 1
                            if has_head(s, 2):
                                maxima(s + 2, before)
                            else:
                                normalise(before)

                        all_steps(dve, step)
                        normalise(BH - 1)

                    @block.gpsimd
                    def _(pool):
                        pool.wait_ge(cleared, 1)

                        def copy_values(head, par):
                            src = VO[:, ds(head, 1), :, :].rearrange("p a t d -> p (a t) d")
                            nc.gpsimd.tensor_copy(vst[par][:, :, 0:HD], src).then_inc(v_copied, 1)

                        def split_max(head):
                            pool.wait_ge(max_steps, head * max_links + max_links)
                            pool.wait_ge(m_turned, head)
                            high, mid, low = (mparts[:, i * NT:(i + 1) * NT] for i in range(3))
                            steps = Linked(pool, split, head * split_links)
                            steps(nc.gpsimd.tensor_tensor(high, negmax[:], zeros[:], ALU.add))
                            steps(nc.gpsimd.tensor_tensor(mrest[:], negmax[:], high, ALU.subtract))
                            steps(nc.gpsimd.tensor_tensor(mid, mrest[:], zeros[:], ALU.add))
                            steps(nc.gpsimd.tensor_tensor(mrest[:], mrest[:], mid, ALU.subtract))
                            steps(nc.gpsimd.tensor_tensor(low, mrest[:], zeros[:], ALU.add))

                        copy_values(0, 0)
                        split_max(0)
                        split_max(1)

                        def step(s, par, half):
                            if has_head(s, 1):
                                if not at_first(s):
                                    pool.wait_ge(pv_done, s * NT)
                                    nc.gpsimd.tensor_tensor(word[:], zeros[:, 0:1], zeros[:, 0:1], ALU.add)
                                copy_values(s + 1, 1 - par)
                            if has_head(s, 2):
                                split_max(s + 2)

                        all_steps(pool, step)

                    @block.scalar
                    def _(act):
                        def copy_acc(head):
                            act.wait_ge(pv_done, head * NT + NT)
                            act.wait_ge(u_turned, head)
                            nc.scalar.activation(u[:], acc[:], ACT.Copy).then_inc(acc_copied, 1)

                        def copy_max_row(head):
                            act.wait_ge(m_turned, head + 1)
                            act.wait_ge(m_in, head * 16)
                            nc.scalar.activation(mrow[:], psM[0:3 * NT, :], ACT.Copy).then_inc(m_row, 1)

                        copy_max_row(0)

                        def step(s, par, half):
                            for n, (i, c0, c1) in enumerate(units2):
                                if i == 1 and units2[n - 1][0] == 0 and not at_first(s):
                                    copy_acc(s - 1)
                                if i == 6 and units2[n - 1][0] == 5 and has_head(s, 1):
                                    copy_max_row(s + 1)
                                act.wait_ge(ready2, s * n2 + (n + 1))
                                if not (at_first(s) and i < pt_bufs):
                                    act.wait_ge(pv_done, s * NT + (i + 1 - pt_bufs))
                                base = c1 - 2 * BANK
                                nc.scalar.activation(pt[i % pt_bufs][:, c0:c1], ps2[n % 2][:, c0 - base:c1 - base],
                                                     ACT.Exp).then_inc(exped, 1)

                        all_steps(act, step)
                        copy_acc(BH - 1)

                    @block.tensor
                    def _(pe):
                        pe.wait_ge(consts, 1)
                        last_unit = {i: n for n, (i, _, _) in enumerate(units2)}

                        def masked(out, lhsT, rhs, mask):
                            if mask is None:
                                return nc.tensor.matmul(out, lhsT, rhs, start=True, stop=True)
                            nc.tensor.matmul(out, lhsT, rhs, start=True, stop=False)
                            cols, m = mask
                            return nc.tensor.matmul(cols, identb[:], maskb[:, m, :], start=False, stop=True)

                        def scores1(head, par, n):
                            i, c0, c1 = units1[n]
                            if not (isinstance(head, int) and head == 0 and n < 2):
                                pe.wait_ge(taken1, head * n1 + (n - 1))
                            out = ps1[n % 2][:, 0:c1 - c0]
                            mask = (out[:, c1 - c0 - P:], 0) if c1 == (i + 1) * P else None
                            masked(out, q1[par][:, i * P:(i + 1) * P], k1[par][:, c0:c1], mask).then_inc(ready1, 1)

                        def scores2(head, par, n):
                            i, c0, c1 = units2[n]
                            if not (at_first(head) and n < 2):
                                pe.wait_ge(exped, head * n2 + (n - 1))
                            base = c1 - 2 * BANK
                            for b0 in range(base, c1, BANK):
                                a0 = max(b0, c0)
                                if a0 >= b0 + BANK:
                                    continue
                                out = ps2[n % 2][:, a0 - base:b0 + BANK - base]
                                mask = (out[:, 0:P], 1) if a0 == i * P else None
                                last = masked(out, k2[par][:, i * P:(i + 1) * P], q2[par][:, a0:b0 + BANK], mask)
                            last.then_inc(ready2, 1)

                        def product(head, par, i):
                            if i == 0:
                                pe.wait_ge(v_copied, head + 1)
                                pe.wait_ge(acc_copied, head)
                            pe.wait_ge(exped, head * n2 + (last_unit[i] + 1))
                            last = None
                            for j in range(CH):
                                mm = times_values(acc, j, vst[par][:, i, :], pt[i % pt_bufs][:], i, (i == 0, i == NT - CH + j))
                                last = mm or last
                            last.then_inc(pv_done, 1)
                            return last

                        def turn_out(head):
                            pe.wait_ge(acc_copied, head + 1)
                            for m in range(CH):
                                last = nc.tensor.transpose(psT[:, m, :], u[:, m * P:(m + 1) * P], identf[:])
                            last.then_inc(u_turned, 1)

                        def turn_max(head):
                            pe.wait_ge(split, head * split_links + split_links)
                            nc.tensor.transpose(psM, mparts[:], identb[:]).then_inc(m_turned, 1)

                        for g in range(2):
                            pe.wait_ge(in1[g], 32)
                            for n in range(n1):
                                scores1(g, g, n)
                        turn_max(0)

                        def step(s, par, half):
                            pe.wait_ge(in2[par], half * 32 + 32)
                            pe.wait_ge(m_in, s * 16 + 16)
                            n = 0
                            for i in range(NT):
                                for m, (tile, _, _) in enumerate(units2):
                                    if tile == i:
                                        scores2(s, par, m)
                                if has_head(s, 2):
                                    if i == 0:
                                        pe.wait_ge(in1[par], half * 32 + 64)
                                    while n < n1 and units1[n][0] == i:
                                        scores1(s + 2, par, n)
                                        n += 1
                                if i >= 1:
                                    product(s, par, i - 1)
                                if i == 2 and not at_first(s):
                                    pe.wait_ge(m_row, s + 1)
                                    turn_out(s - 1)
                                if i == 5 and has_head(s, 1):
                                    if at_first(s):
                                        pe.wait_ge(m_row, 1)
                                    else:
                                        pe.wait_ge(normalised, s)
                                    turn_max(s + 1)
                            product(s, par, NT - 1)

                        all_steps(pe, step)
                        pe.wait_ge(normalised, BH - 1)
                        turn_out(BH - 1)

        def out_project_stage(name, w_name, b_name, load_x=False):
            with ExitStack() as ctx:
                def sem(n):
                    return ctx.enter_context(nc.semaphore(f"{name}_{n}"))

                w = sb(f"{name}_w", [P, KC, C], ctx=ctx)
                bias = sb(f"{name}_bias", [P, C], ctx=ctx)
                gathered = sb(f"{name}_gathered", [P, CH, C], ctx=ctx)
                oT = sb(f"{name}_oT", [P, KC, CW], ctx=ctx)
                st = stats_scratch(name, ctx)
                psT = ps(f"{name}_psT", [P, KC, CW], ctx=ctx)
                psY = ps(f"{name}_psY", [P, CH, C], ctx=ctx)
                w_in, by_token, turned, oT_ready = sem("w_in"), sem("by_token"), sem("turned"), sem("oT_ready")
                y_ready, added, stat_steps, x_back = sem("y_ready"), sem("added"), sem("stat_steps"), sem("x_back")
                n_in = 16 + (16 if b_name else 0)
                with nc.Block() as block:
                    @block.sync
                    def _(sp):
                        sp.dma_start(w[:], io[w_name].rearrange("(k p) n -> p k n", p=P)).then_inc(w_in, 16)
                        if b_name:
                            sp.dma_start(bias[:], io[b_name]).then_inc(w_in, 16)
                        if load_x:
                            for n in range(B * NCH):
                                b, t0 = n // NCH, n % NCH * CW
                                sp.dma_start(X[:, n * CH:(n + 1) * CH, :],
                                             x_kept[b, t0:t0 + CW, :].rearrange("(t p) c -> p t c", p=P)).then_inc(x_back, 16)

                    @block.scalar
                    def _(act):
                        with act.Fori(0, B) as b:
                            with act.Fori(0, NCH) as c:
                                n = b * NCH + c
                                act.wait_ge(turned, n)
                                for t in range(CH):
                                    src = VO_tiles[:, ds(b, 1), :, ds(c * CH + t, 1), :].rearrange("p a h t d -> p (a h) (t d)")
                                    last = nc.scalar.activation(gathered[:, t, :].rearrange("p (h d) -> p h d", h=H), src, ACT.Copy)
                                last.then_inc(by_token, 1)

                    @block.tensor
                    def _(pe):
                        pe.wait_ge(w_in, n_in)
                        with pe.Fori(0, B * NCH) as n:
                            pe.wait_ge(by_token, n + 1)
                            pe.wait_ge(oT_ready, n)
                            for t in range(CH):
                                for k in range(KC):
                                    last = nc.tensor.transpose(psT[:, k, t * P:(t + 1) * P], gathered[:, t, k * P:(k + 1) * P], identf[:])
                            last.then_inc(turned, 1)
                            pe.wait_ge(oT_ready, n + 1)
                            pe.wait_ge(added, n)
                            for t in range(CH):
                                for k in range(KC):
                                    last = nc.tensor.matmul(psY[:, t, :], oT[:, k, t * P:(t + 1) * P], w[:, k, :],
                                                            start=(k == 0), stop=(k == KC - 1))
                            last.then_inc(y_ready, 1)

                    @block.vector
                    def _(dve):
                        dve.wait_ge(w_in, n_in)
                        with dve.Fori(0, B * NCH) as n:
                            per_chunk = CHUNK_STEPS + (1 if b_name else 0)
                            link = Linked(dve, stat_steps, n * per_chunk)
                            x_chunk = X[:, ds(n * CH, CH), :]
                            dve.wait_ge(turned, n + 1)
                            dve.wait_ge(y_ready, n)
                            nc.vector.tensor_copy(oT[:], psT[:]).then_inc(oT_ready, 1)
                            if load_x:
                                dve.wait_ge(x_back, B * NCH * 16)
                            if b_name:
                                link(nc.vector.tensor_tensor(x_chunk, x_chunk, bias[:].unsqueeze(1).broadcast_to([P, CH, C]), ALU.add))
                            dve.wait_ge(y_ready, n + 1)
                            nc.vector.tensor_tensor(x_chunk, psY[:], x_chunk, ALU.add).then_inc(added, 1)
                            dve.wait_ge(added, n + 1)
                            chunk_stats(link, n, st)

        def ffn_stage(name):
            HALF = NE // 2
            with ExitStack() as ctx:
                def sem(n):
                    return ctx.enter_context(nc.semaphore(f"{name}_{n}"))

                ew = sb(f"{name}_ew", [P, KC, NE, C], ctx=ctx)
                eb = sb(f"{name}_eb", [NE, C], ctx=ctx)
                rw = sb(f"{name}_rw", [P, KC, NE], ctx=ctx)
                rb = sb(f"{name}_rb", [P, NE], ctx=ctx)
                countdown = sb(f"{name}_countdown", [P, NE], ctx=ctx)
                xn = sb(f"{name}_xn", [P, CH, C], ctx=ctx)
                xnT = [sb(f"{name}_xnT{i}", [P, KC, CW], ctx=ctx) for i in range(2)]
                logit = sb(f"{name}_logit", [P, CH, NE], ctx=ctx)
                prob = sb(f"{name}_prob", [P, CH, NE], ctx=ctx)
                hit = sb(f"{name}_hit", [P, CH, NE], ctx=ctx)
                gate = sb(f"{name}_gate", [P, CH, NE], ctx=ctx)
                top = sb(f"{name}_top", [P, CH], ctx=ctx)
                total = sb(f"{name}_total", [P, CH], ctx=ctx)
                gateT = sb(f"{name}_gateT", [NE, CH, P], ctx=ctx)
                st = stats_scratch(name, ctx)
                psT = ps(f"{name}_psT", [P, KC, CW], ctx=ctx)
                psL = psT[:, 0, 0:CH * NE].rearrange("p (t e) -> p t e", e=NE)
                psG = psT[0:NE, 1, :].rearrange("p (t n) -> p t n", t=CH)
                psB = ps(f"{name}_psB", [P, CH, C], ctx=ctx)
                psE = [ps(f"{name}_psE{i}", [P, HALF, C], ctx=ctx) for i in range(2)]
                w_in, normed, turned, xnT_ready = sem("w_in"), sem("normed"), sem("turned"), sem("xnT_ready")
                logits_ready, shifted, exped = sem("logits_ready"), sem("shifted"), sem("exped")
                gated, gates_turned, gateT_ready = sem("gated"), sem("gates_turned"), sem("gateT_ready")
                bias_ready, e_ready = sem("bias_ready"), sem("e_ready")
                router_steps, x_steps = sem("router_steps"), sem("x_steps")
                n_chunks, units = B * NCH, 2 * CH
                router_links, x_links = 10, 1 + CH * NE + CHUNK_STEPS

                def used_at(u):
                    return HALF * (u % units + 1) + (1 if u % units >= 2 else 0) - (x_links if u < 0 else 0)

                def over_experts(ap):
                    return ap.unsqueeze(2).broadcast_to([P, CH, NE])

                def over_tokens(ap):
                    return ap.unsqueeze(1).broadcast_to([P, CH, NE])

                with nc.Block() as block:
                    @block.sync
                    def _(sp):
                        for k in range(KC):
                            sp.dma_start(ew[:, k, :, :], io["expert_w"][:, k * P:(k + 1) * P, :].rearrange("e p d -> p e d")).then_inc(w_in, 16)
                        sp.dma_start(eb[:], io["expert_b"]).then_inc(w_in, 16)
                        sp.dma_start(rw[:], io["router_w"].rearrange("(k p) n -> p k n", p=P)).then_inc(w_in, 16)
                        sp.dma_start(rb[:], io["router_b"]).then_inc(w_in, 16)
                        sp.dma_start(countdown[:], io["countdown"]).then_inc(w_in, 16)

                    @block.scalar
                    def _(act):
                        def copy_turned(n, par):
                            act.wait_ge(turned, n + 1)
                            nc.scalar.activation(xnT[par][:], psT[:], ACT.Copy).then_inc(xnT_ready, 1)

                        def chunk(n, par, more):
                            act.wait_ge(shifted, n + 1)
                            nc.scalar.activation(prob[:], logit[:], ACT.Exp).then_inc(exped, 1)
                            act.wait_ge(gates_turned, n + 1)
                            nc.scalar.activation(gateT[:], psG, ACT.Copy).then_inc(gateT_ready, 1)
                            if more:
                                copy_turned(n + 1, 1 - par)

                        copy_turned(0, 0)
                        with act.Fori(0, n_chunks // 2 - 1) as k:
                            for par in range(2):
                                chunk(k * 2 + par, par, True)
                        chunk(n_chunks - 2, 0, True)
                        chunk(n_chunks - 1, 1, False)

                    @block.tensor
                    def _(pe):
                        pe.wait_ge(w_in, 96)

                        def turn(n):
                            for t in range(CH):
                                pe.wait_ge(normed, n * CH + (t + 1))
                                for k in range(KC):
                                    last = nc.tensor.transpose(psT[:, k, t * P:(t + 1) * P], xn[:, t, k * P:(k + 1) * P], identf[:])
                            last.then_inc(turned, 1)

                        def expert_unit(n, par, u):
                            t, half = u // 2, u % 2
                            if not (isinstance(n, int) and n == 0 and u < 2):
                                pe.wait_ge(x_steps, n * x_links + used_at(u - 2))
                            for pair in range(0, HALF, 2):
                                for k in range(KC):
                                    e = half * HALF + pair
                                    last = nc.tensor.matmul(psE[u % 2][:, pair:pair + 2, :], xnT[par][:, k, t * P:(t + 1) * P],
                                                            ew[:, k, e:e + 2, :], start=(k == 0), stop=(k == KC - 1))
                            last.then_inc(e_ready, 1)

                        def chunk(n, par, more):
                            pe.wait_ge(xnT_ready, n + 1)
                            for t in range(CH):
                                for k in range(KC):
                                    last = nc.tensor.matmul(psL[:, t, :], xnT[par][:, k, t * P:(t + 1) * P], rw[:, k, :],
                                                            start=(k == 0), stop=(k == KC - 1))
                            last.then_inc(logits_ready, 1)
                            for u in range(2):
                                expert_unit(n, par, u)
                            pe.wait_ge(gated, n + 1)
                            for t in range(CH):
                                last = nc.tensor.transpose(psG[:, t, :], gate[:, t, :], identf[:])
                            last.then_inc(gates_turned, 1)
                            expert_unit(n, par, 2)
                            pe.wait_ge(gateT_ready, n + 1)
                            for t in range(CH):
                                last = nc.tensor.matmul(psB[:, t, :], gateT[:, t, :], eb[:], start=True, stop=True)
                            last.then_inc(bias_ready, 1)
                            for u in range(3, units):
                                if u == 5 and more:
                                    turn(n + 1)
                                expert_unit(n, par, u)

                        turn(0)
                        chunk(0, 0, True)
                        chunk(1, 1, True)
                        with pe.Fori(1, n_chunks // 2 - 1) as k:
                            for par in range(2):
                                chunk(k * 2 + par, par, True)
                        chunk(n_chunks - 2, 0, True)
                        chunk(n_chunks - 1, 1, False)

                    @block.vector
                    def _(dve):
                        dve.wait_ge(w_in, 96)

                        def normalise(n):
                            dve.wait_ge(turned, n)
                            for t in range(CH):
                                normalise_tile(xn[:, t, :], n * CH + t).then_inc(normed, 1)

                        def route(n):
                            link = Linked(dve, router_steps, n * router_links)
                            dve.wait_ge(logits_ready, n + 1)
                            link(nc.vector.tensor_tensor(logit[:], psL, over_tokens(rb[:]), ALU.add))
                            link(nc.vector.tensor_reduce(top[:], logit[:], AX, ALU.max))
                            nc.vector.tensor_tensor(logit[:], logit[:], over_experts(top[:]), ALU.subtract).then_inc(shifted, 1)
                            dve.wait_ge(exped, n + 1)
                            link(nc.vector.tensor_reduce(total[:], prob[:], AX, ALU.add))
                            link(nc.vector.reciprocal(total[:], total[:]))
                            link(nc.vector.tensor_tensor(prob[:], prob[:], over_experts(total[:]), ALU.mult))
                            link(nc.vector.tensor_reduce(top[:], prob[:], AX, ALU.max))
                            link(nc.vector.tensor_tensor(hit[:], prob[:], over_experts(top[:]), ALU.is_equal))
                            link(nc.vector.tensor_tensor(hit[:], hit[:], over_tokens(countdown[:]), ALU.mult))
                            link(nc.vector.tensor_reduce(top[:], hit[:], AX, ALU.max))
                            link(nc.vector.tensor_tensor(hit[:], hit[:], over_experts(top[:]), ALU.is_equal))
                            nc.vector.tensor_tensor(gate[:], hit[:], prob[:], ALU.mult).then_inc(gated, 1)
                            dve.wait_ge(gated, n + 1)

                        def chunk(n, more):
                            route(n)
                            link = Linked(dve, x_steps, n * x_links)
                            for u in range(units):
                                t, half = u // 2, u % 2
                                if u == 2:
                                    dve.wait_ge(bias_ready, n + 1)
                                    x_chunk = X[:, ds(n * CH, CH), :]
                                    link(nc.vector.tensor_tensor(x_chunk, psB[:], x_chunk, ALU.add))
                                dve.wait_ge(e_ready, n * units + (u + 1))
                                x_tile = X[:, ds(n * CH + t, 1), :].rearrange("p a n -> p (a n)")
                                for e in range(HALF):
                                    g = half * HALF + e
                                    link(nc.vector.scalar_tensor_tensor(x_tile, psE[u % 2][:, e, :], gate[:, t, g:g + 1],
                                                                        x_tile, ALU.mult, ALU.add))
                                if u == 3 and more:
                                    normalise(n + 1)
                            chunk_stats(link, n, st)

                        normalise(0)
                        with dve.Fori(0, n_chunks - 1) as n:
                            chunk(n, True)
                        chunk(n_chunks - 1, False)

        def project_b_stage():
            with ExitStack() as ctx:
                def sem(name):
                    return ctx.enter_context(nc.semaphore("pb_" + name))

                HB = 2 * C // P
                w = sb("pb_w", [P, KC, 3 * C], ctx=ctx)
                bias = sb("pb_bias", [P, 3 * C], ctx=ctx)
                xn = sb("pb_xn", [P, CH, C], ctx=ctx)
                xnT = sb("pb_xnT", [P, KC, CW], ctx=ctx)
                qk = sb("pb_qk", [P, CH, 2 * C], ctx=ctx)
                square = sb("pb_square", [P, CH, 2 * C], ctx=ctx)
                norm = sb("pb_norm", [P, CH * 2 * H], ctx=ctx)
                rest = sb("pb_rest", [P, HB, CW], ctx=ctx)
                part = [sb(f"pb_part{i}", [P, HB, CW], BF16, ctx=ctx) for i in range(3)]
                psT = ps("pb_psT", [P, KC, CW], ctx=ctx)
                psQK = [ps(f"pb_psQK{i}", [P, 2 * C], ctx=ctx) for i in range(2)]
                psR = ps("pb_psR", [P, HB, CW], ctx=ctx)
                psV = psT[:].rearrange("p k (t n) -> p (k t) n", n=C)
                w_in, normed, turned, xnT_ready = sem("w_in"), sem("normed"), sem("turned"), sem("xnT_ready")
                qk_ready, qk_taken, v_ready, v_taken = sem("qk_ready"), sem("qk_taken"), sem("v_ready"), sem("v_taken")
                squared, summed, rooted, norm_steps = sem("squared"), sem("summed"), sem("rooted"), sem("norm_steps")
                unit_ready, unit_turned, x_stored = sem("unit_ready"), sem("unit_turned"), sem("x_stored")
                high, rested, mid, rested2, low, stored = (sem(x) for x in ("high", "rested", "mid", "rested2", "low", "stored"))
                n_stores = 3 * HB
                with nc.Block() as block:
                    @block.sync
                    def _(sp):
                        sp.dma_start(w[:], io["w_qkv"].rearrange("(k p) n -> p k n", p=P)).then_inc(w_in, 16)
                        sp.dma_start(bias[:], io["b_qkv"]).then_inc(w_in, 16)
                        for b in range(B):
                            sp.dma_start(x_kept[b].rearrange("(t p) c -> p t c", p=P), X[:, b * NT:(b + 1) * NT, :]).then_inc(x_stored, 16)
                        with sp.Fori(0, B) as b:
                            with sp.Fori(0, NCH) as c:
                                n = b * NCH + c
                                for i, made in enumerate((high, mid, low)):
                                    sp.wait_ge(made, n + 1)
                                    for blk in range(HB):
                                        side, heads = "qk"[blk // 2], (blk % 2) * (H // 2)
                                        dst = parts_b[side][ds(b * H + heads, H // 2), i, :, ds(c * CW, CW)]
                                        sp.dma_start(dst, part[i][:, blk, :]).then_inc(stored, 16)
                        sp.wait_ge(stored, B * NCH * n_stores * 16)
                        sp.wait_ge(x_stored, B * 16)

                    @block.scalar
                    def _(act):
                        with act.Fori(0, B * NCH) as n:
                            act.wait_ge(turned, n + 1)
                            nc.scalar.activation(xnT[:], psT[:], ACT.Copy).then_inc(xnT_ready, 1)
                            act.wait_ge(qk_taken, n * CH + CH)
                            nc.scalar.activation(square[:], qk[:], ACT.Square).then_inc(squared, 1)
                            act.wait_ge(summed, n + 1)
                            nc.scalar.activation(norm[:], norm[:], ACT.Sqrt).then_inc(rooted, 1)
                            act.wait_ge(unit_turned, n + 1)
                            act.wait_ge(stored, n * (n_stores * 16))
                            nc.scalar.activation(part[0][:], psR[:], ACT.Copy).then_inc(high, 1)
                            act.wait_ge(rested, n + 1)
                            nc.scalar.activation(part[1][:], rest[:], ACT.Copy).then_inc(mid, 1)

                    @block.gpsimd
                    def _(pool):
                        with pool.Fori(0, B * NCH) as n:
                            pool.wait_ge(mid, n + 1)
                            nc.gpsimd.tensor_tensor(part[2][:], rest[:], part[1][:], ALU.subtract).then_inc(low, 1)

                    @block.tensor
                    def _(pe):
                        pe.wait_ge(w_in, 32)

                        with pe.Fori(0, B * NCH) as n:
                            pe.wait_ge(v_taken, n * CH)
                            for t in range(CH):
                                pe.wait_ge(normed, n * CH + (t + 1))
                                for k in range(KC):
                                    last = nc.tensor.transpose(psT[:, k, t * P:(t + 1) * P], xn[:, t, k * P:(k + 1) * P], identf[:])
                            last.then_inc(turned, 1)
                            pe.wait_ge(xnT_ready, n + 1)
                            for t in range(CH):
                                pe.wait_ge(qk_taken, n * CH + max(t - 1, 0))
                                for k in range(KC):
                                    last = nc.tensor.matmul(psQK[t % 2][:], xnT[:, k, t * P:(t + 1) * P], w[:, k, 0:2 * C],
                                                            start=(k == 0), stop=(k == KC - 1))
                                last.then_inc(qk_ready, 1)
                            for t in range(CH):
                                for k in range(KC):
                                    last = nc.tensor.matmul(psV[:, t, :], xnT[:, k, t * P:(t + 1) * P], w[:, k, 2 * C:3 * C],
                                                            start=(k == 0), stop=(k == KC - 1))
                            last.then_inc(v_ready, 1)
                            pe.wait_ge(unit_ready, n + 1)
                            pe.wait_ge(rested, n)
                            for blk in range(HB):
                                for t in range(CH):
                                    last = nc.tensor.transpose(psR[:, blk, t * P:(t + 1) * P], qk[:, t, blk * P:(blk + 1) * P], identf[:])
                            last.then_inc(unit_turned, 1)

                    @block.vector
                    def _(dve):
                        dve.wait_ge(w_in, 32)
                        with dve.Fori(0, B) as b:
                            with dve.Fori(0, NCH) as c:
                                n = b * NCH + c
                                dve.wait_ge(turned, n)
                                for t in range(CH):
                                    normalise_tile(xn[:, t, :], n * CH + t).then_inc(normed, 1)
                                dve.wait_ge(unit_turned, n)
                                for t in range(CH):
                                    dve.wait_ge(qk_ready, n * CH + (t + 1))
                                    nc.vector.tensor_tensor(qk[:, t, :], psQK[t % 2][:], bias[:, 0:2 * C], ALU.add).then_inc(qk_taken, 1)
                                dve.wait_ge(v_ready, n + 1)
                                for t in range(CH):
                                    dst = VO_tiles[:, ds(b, 1), :, ds(c * CH + t, 1), :].rearrange("p a h t d -> p (a h) (t d)")
                                    nc.vector.tensor_tensor(dst, psV[:, t, :].rearrange("p (h d) -> p h d", h=H),
                                                            bias[:, 2 * C:].rearrange("p (h d) -> p h d", h=H), ALU.add).then_inc(v_taken, 1)
                                link = Linked(dve, norm_steps, n * 2)
                                dve.wait_ge(squared, n + 1)
                                nc.vector.tensor_reduce(norm[:], square[:].rearrange("p t (h d) -> p (t h) d", d=HD), AX, ALU.add).then_inc(summed, 1)
                                dve.wait_ge(rooted, n + 1)
                                link(nc.vector.tensor_scalar(norm[:], norm[:], 1e-12, None, ALU.max))
                                link(nc.vector.reciprocal(norm[:], norm[:]))
                                qk_heads = qk[:].rearrange("p t (h d) -> p (t h) d", d=HD)
                                nc.vector.tensor_tensor(qk_heads, qk_heads, norm[:].unsqueeze(2).broadcast_to([P, CH * 2 * H, HD]),
                                                        ALU.mult).then_inc(unit_ready, 1)
                                dve.wait_ge(high, n + 1)
                                dve.wait_ge(low, n)
                                nc.vector.tensor_tensor(rest[:], psR[:], part[0][:], ALU.subtract).then_inc(rested, 1)

        def attention_b_stage():
            UNIT = 2 * BANK
            per_tile, per_pair = T // UNIT, 2 * T // UNIT
            n_units = NT * per_tile
            pool_pairs = [p for p in range(PAIRS) if p not in DVE_SQUARES]
            q_runs = [(0, 3), (1, 2), (2, 1)]
            k_runs = [3, 2, 1]
            K1 = HD * sum(terms for _, terms in q_runs)
            K2 = K1 + 1
            with ExitStack() as ctx:
                def sem(name):
                    return ctx.enter_context(nc.semaphore("ab_" + name))

                f = sb("ab_f", [P, NT, T], ctx=ctx)
                qs = sb("ab_qs", [P, T], BF16, ctx=ctx)
                ks = sb("ab_ks", [P, T], BF16, ctx=ctx)
                neg = sb("ab_neg", [P, NT, T], mybir.dt.uint8, ctx=ctx)
                two = sb("ab_two", [P, P], mybir.dt.uint8, ctx=ctx)
                ncol = sb("ab_ncol", [P, NT], ctx=ctx)
                rcol = sb("ab_rcol", [P, NT], ctx=ctx)
                vst = sb("ab_vst", [P, NT, 32], ctx=ctx)
                u = sb("ab_u", [P, BANK], ctx=ctx)
                least = sb("ab_least", [P, CH, CH], ctx=ctx)
                rsum = sb("ab_rsum", [P, CH, CH], ctx=ctx)
                psC = [ps(f"ab_psC{i}", [P, UNIT], ctx=ctx) for i in range(PSC)]
                acc = ps("ab_acc", [P, BANK], ctx=ctx)
                psT = ps("ab_psT", [P, CH, P], ctx=ctx)
                u_view = psT[:].rearrange("p m (j e) -> p m j e", j=CH)
                two8 = two[:].bitcast(mybir.dt.float8e4)
                neg8 = neg[:].bitcast(mybir.dt.float8e4)
                cleared, stacks_in = sem("cleared"), sem("stacks_in")
                c_ready, c_taken = sem("c_ready"), sem("c_taken")
                squared_pool, squared_dve = sem("squared_pool"), sem("squared_dve")
                rooted, arctaned, logged = sem("rooted"), sem("arctaned"), sem("logged")
                neg_ready, halved = sem("neg_ready"), sem("halved")
                f_ready = sem("f_ready")
                scale_steps, scaled, pv_done = sem("scale_steps"), sem("scaled"), sem("pv_done")
                acc_copied, u_turned, out_steps = sem("acc_copied"), sem("u_turned"), sem("out_steps")
                n_loads, out_links = 16 * (len(q_runs) + len(k_runs)), 4

                def head_units(head):
                    return head * (2 * n_units)

                def all_heads(eng, step):
                    with eng.Fori(0, BH - 1) as h:
                        step(h, True)
                    step(BH - 1, False)

                with nc.Block() as block:
                    @block.sync
                    def _(sp):
                        def load(head):
                            row = 0
                            for part, terms in q_runs:
                                src = parts_b["q"][ds(head, 1), part].broadcast_to([terms, HD, T])
                                sp.dma_start(qs[row:row + terms * HD, :],
                                             src).then_inc(stacks_in, 16)
                                row += terms * HD
                            row = 0
                            for terms in k_runs:
                                src = parts_b["k"][ds(head, 1), 0:terms].rearrange("a e d t -> (a e d) t")
                                sp.dma_start(ks[row:row + terms * HD, :], src).then_inc(stacks_in, 16)
                                row += terms * HD

                        sp.wait_ge(cleared, 2)
                        load(0)
                        with sp.Fori(0, BH - 1) as h:
                            sp.wait_ge(c_ready, head_units(h + 1))
                            load(h + 1)

                    @block.tensor
                    def _(pe):
                        def unit(head, second, n):
                            at = second * n_units + n
                            before = n - PSC if n >= PSC else max(m for m in range(n_units) if m % PSC == n) - n_units
                            if not (isinstance(head, int) and head == 0 and at + before - n < 0):
                                pe.wait_ge(c_taken, head_units(head) + (at + before - n + 1))
                            i, half = n // per_tile, n % per_tile
                            rows = K2 if second else K1
                            if second and n % per_pair == 0:
                                pe.wait_ge(neg_ready, head * PAIRS + (n // per_pair + 1))
                            for c in range(0, UNIT, BANK):
                                q0 = half * UNIT + c
                                last = nc.tensor.matmul(psC[n % PSC][:, c:c + BANK], ks[0:rows, i * P:(i + 1) * P], qs[0:rows, q0:q0 + BANK],
                                                        start=True, stop=not second)
                            for c in range(0, UNIT if second else 0, BANK):
                                q0 = half * UNIT + c
                                last = nc.tensor.matmul(psC[n % PSC][:, c:c + BANK], two8, neg8[:, i, q0:q0 + BANK],
                                                        start=False, stop=True)
                            last.then_inc(c_ready, 1)

                        def first_units(head, p, some=range(per_pair)):
                            if p == 0:
                                pe.wait_ge(stacks_in, head * n_loads + n_loads)
                            for m in some:
                                unit(head, 0, p * per_pair + m)

                        def product(head, i):
                            if i == 0:
                                pe.wait_ge(acc_copied, head)
                            if i % 2 == 0:
                                pe.wait_ge(scaled, head * PAIRS + (i // 2 + 1))
                            for j in range(CH):
                                last = times_values(acc, j, vst[:, i, :], f[:, i, :], 0, (i == 0, i == NT - 1))
                            if i % 2 == 1:
                                last.then_inc(pv_done, 1)

                        def step(head, has_next):
                            for n in range(n_units):
                                unit(head, 1, n)
                            for p in range(PAIRS):
                                if has_next and p > 0:
                                    first_units(head + 1, p - 1, range(PSC))
                                product(head, 2 * p)
                                if has_next and p > 0:
                                    first_units(head + 1, p - 1, range(PSC, per_pair))
                                product(head, 2 * p + 1)
                            if has_next:
                                first_units(head + 1, PAIRS - 1)
                            pe.wait_ge(acc_copied, head + 1)
                            pe.wait_ge(out_steps, head * out_links)
                            for m in range(CH):
                                last = nc.tensor.transpose(psT[:, m, :], u[:, m * P:(m + 1) * P], identf[:])
                            last.then_inc(u_turned, 1)

                        for p in range(PAIRS):
                            first_units(0, p)
                        all_heads(pe, step)

                    @block.vector
                    def _(dve):
                        nc.vector.memset(vst[:], 0.0).then_inc(cleared, 1)
                        dve.wait_ge(cleared, 1)
                        nc.vector.memset(vst[:, :, HD + 1], 1.0)
                        nc.vector.memset(ks[K1:K1 + 32, :], -1.0)
                        nc.vector.memset(qs[K1:K1 + 32, :], 1.0)
                        nc.vector.tensor_scalar(two[:], identf[:], TWO8, None, ALU.mult).then_inc(cleared, 1)

                        def clip_pair(head, p):
                            for m in range(per_pair):
                                n = p * per_pair + m
                                i, q0 = n // per_tile, n % per_tile * UNIT
                                dve.wait_ge(c_ready, head_units(head) + (n + 1))
                                nc.vector.tensor_scalar(f[:, i, q0:q0 + UNIT], psC[n % PSC][:], CLIP, -CLIP,
                                                        ALU.min, ALU.max).then_inc(c_taken, 1)
                            dve.wait_ge(c_taken, head_units(head) + (p + 1) * per_pair)
                            pair = f[:, 2 * p:2 * p + 2, :]
                            nc.vector.tensor_scalar(neg[:, 2 * p:2 * p + 2, :], pair, 0.0, ONE8, ALU.is_lt, ALU.mult).then_inc(neg_ready, 1)
                            if p in DVE_SQUARES:
                                dve.wait_ge(neg_ready, head * PAIRS + (p + 1))
                                nc.vector.tensor_tensor(pair, pair, pair, ALU.mult).then_inc(squared_dve, 1)

                        def tangent_pair(head, p):
                            dve.wait_ge(rooted, head * PAIRS + (p + 1))
                            for n in range(p * per_pair, (p + 1) * per_pair):
                                i, q0 = n // per_tile, n % per_tile * UNIT
                                dve.wait_ge(c_ready, head_units(head) + (n_units + n + 1))
                                place = f[:, i, q0:q0 + UNIT]
                                nc.vector.tensor_tensor(place, psC[n % PSC][:], place, ALU.mult).then_inc(c_taken, 1)

                        def half_angle(head, p):
                            dve.wait_ge(arctaned, head * PAIRS + (p + 1))
                            pair = f[:, 2 * p:2 * p + 2, :]
                            nc.vector.scalar_tensor_tensor(pair, neg[:, 2 * p:2 * p + 2, :], float(np.pi) / 2 / ONE8, pair,
                                                           ALU.mult, ALU.subtract).then_inc(halved, 1)

                        def scale_values(head, p):
                            two = slice(2 * p, 2 * p + 2)
                            dve.wait_ge(f_ready, head * NT + (2 * p + 2))
                            nc.vector.reciprocal(rcol[:, two], ncol[:, two]).then_inc(scale_steps, 1)
                            dve.wait_ge(scale_steps, head * PAIRS + (p + 1))
                            nc.vector.tensor_copy(vst[:, two, HD], rcol[:, two])
                            values = VO[:, ds(head, 1), two, :].rearrange("p a t d -> p (a t) d")
                            nc.vector.tensor_tensor(vst[:, two, 0:HD], values, rcol[:, two].unsqueeze(2).broadcast_to([P, 2, HD]),
                                                    ALU.mult).then_inc(scaled, 1)

                        def step(head, has_next):
                            for p in range(PAIRS):
                                tangent_pair(head, p)
                            for p in range(AHEAD):
                                half_angle(head, p)
                            for p in range(PAIRS):
                                if p + AHEAD < PAIRS:
                                    half_angle(head, p + AHEAD)
                                scale_values(head, p)
                                if has_next and p > 0:
                                    dve.wait_ge(pv_done, head * PAIRS + p)
                                    clip_pair(head + 1, p - 1)
                            dve.wait_ge(pv_done, head * PAIRS + PAIRS)
                            dve.wait_ge(u_turned, head)
                            nc.vector.tensor_copy(u[:], acc[:]).then_inc(acc_copied, 1)
                            if has_next:
                                clip_pair(head + 1, PAIRS - 1)
                            link = Linked(dve, out_steps, head * out_links)
                            dve.wait_ge(u_turned, head + 1)
                            link(nc.vector.tensor_scalar(least[:], u_view[:, :, :, HD + 1], 1e-12, None, ALU.mult))
                            link(nc.vector.tensor_tensor(rsum[:], u_view[:, :, :, HD], least[:], ALU.max))
                            link(nc.vector.reciprocal(rsum[:], rsum[:]))
                            link(nc.vector.tensor_tensor(head_out(head), u_view[:, :, :, 0:HD],
                                                         rsum[:].unsqueeze(3).broadcast_to([P, CH, CH, HD]), ALU.mult))

                        for p in range(PAIRS):
                            clip_pair(0, p)
                        all_heads(dve, step)

                    @block.gpsimd
                    def _(pool):
                        with pool.Fori(0, BH) as h:
                            for p in pool_pairs:
                                pool.wait_ge(neg_ready, h * PAIRS + (p + 1))
                                pair = f[:, 2 * p:2 * p + 2, :].rearrange("p a t -> p (a t)")
                                nc.gpsimd.tensor_tensor(pair, pair, pair, ALU.mult).then_inc(squared_pool, 1)

                    @block.scalar
                    def _(act):
                        def pair_of(p):
                            return f[:, 2 * p:2 * p + 2, :].rearrange("p a t -> p (a t)")

                        with act.Fori(0, BH) as h:
                            for p in range(PAIRS):
                                if p in DVE_SQUARES:
                                    act.wait_ge(squared_dve, h * len(DVE_SQUARES) + (DVE_SQUARES.index(p) + 1))
                                else:
                                    act.wait_ge(squared_pool, h * len(pool_pairs) + (pool_pairs.index(p) + 1))
                                nc.scalar.activation(pair_of(p), pair_of(p), ACT.Abs_reciprocal_sqrt, bias=1.0, scale=-1.0).then_inc(rooted, 1)
                            for p in range(PAIRS):
                                act.wait_ge(c_taken, head_units(h) + (n_units + (p + 1) * per_pair))
                                nc.scalar.activation(pair_of(p), pair_of(p), ACT.Arctan).then_inc(arctaned, 1)
                            nc.scalar.preload_act_table_set("natural_log_exp_and_others")

                            def log_pair(p):
                                act.wait_ge(halved, h * PAIRS + (p + 1))
                                nc.scalar.activation(pair_of(p), pair_of(p), ACT.Ln, bias=1.0, scale=2.0).then_inc(logged, 1)

                            log_pair(0)
                            for p in range(PAIRS):
                                if p + 1 < PAIRS:
                                    log_pair(p + 1)
                                act.wait_ge(logged, h * PAIRS + (p + 1))
                                for i in (2 * p, 2 * p + 1):
                                    nc.scalar.activation(f[:, i, :], f[:, i, :], ACT.Exp, scale=POWER,
                                                         accum_out=ncol[:, i:i + 1]).then_inc(f_ready, 1)

        stages = [
            load_stage, lambda: rstd_stage("ln1"), project_a_stage, attention_a_stage,

            lambda: out_project_stage("oa", "wo", None), lambda: rstd_stage("ln2"), lambda: ffn_stage("f1"),
            lambda: rstd_stage("ln3"), project_b_stage, attention_b_stage,
            lambda: out_project_stage("ob", "w_out", "b_out", load_x=True), lambda: rstd_stage("ln4"), lambda: ffn_stage("f2"),
        ]
        for n, stage in enumerate(stages):
            if n <= last_stage:
                if stage is attention_b_stage:
                    x_place.close()
                stage()
                if stage is attention_b_stage:
                    X = place_x("X_again")
        with ExitStack() as ctx:
            out_done = ctx.enter_context(nc.semaphore("out_done"))
            with nc.Block() as block:
                @block.sync
                def _(sp):
                    for b in range(B):
                        sp.dma_start(io["out"][b].rearrange("(t p) c -> p t c", p=P),
                                     X[:, b * NT:(b + 1) * NT, :]).then_inc(out_done, 16)
                    sp.wait_ge(out_done, 16 * B)
        x_place.close()


def device_inputs(inputs):
    g = {k: np.asarray(v) for k, v in inputs.items()}
    f = np.float32
    wq, wk = g["L0_attn_a_wq"], g["L0_attn_a_wk"]
    wqk = np.zeros((C, 112), f)
    wqk[:, 0:48], wqk[:, 64:112] = wq, wk
    spread = np.zeros((112, P), f)
    for half in (0, 64):
        for h in range(H):
            for d in range(3):
                spread[half + 3 * h + d, half + A_D * h + d] = 1.0
                spread[half + 3 * h + d, half + A_D * h + 3] = g["L0_attn_a_head_dirs"][h, d]
    qscale = np.ones((P, 1), f)
    for h in range(H):
        qscale[A_D * h:A_D * h + 3, 0] = g["L0_attn_a_scale"][0]
    row, col = np.indices((P, P))
    upper = np.where(col > row, MASKED, 0.0).astype(f)
    lower = np.where(row > col, MASKED, 0.0).astype(f)
    spread_over = lambda a: np.ascontiguousarray(np.broadcast_to(a, (P, a.size)))
    return {
        "x": g["L0_attn_a_x"], "wqk": wqk, "wv": g["L0_attn_a_wv"], "wo": g["L0_attn_a_wo"],
        "spread": spread, "qscale": qscale, "ident": np.eye(P, dtype=f), "masks": np.stack([upper, lower]),
        "w_qkv": np.ascontiguousarray(g["L0_attn_b_w_qkv"].T), "b_qkv": spread_over(g["L0_attn_b_b_qkv"]),
        "w_out": np.ascontiguousarray(g["L0_attn_b_w_out"].T), "b_out": spread_over(g["L0_attn_b_b_out"]),
        "router_w": g["L0_ffn_router_w"], "router_b": spread_over(g["L0_ffn_router_b"]),
        "countdown": spread_over(np.arange(NE, 0, -1).astype(f)),
        "expert_w": g["L0_ffn_expert_w"], "expert_b": g["L0_ffn_expert_b"],
    }


def program(nc, arrays, last_stage=99):
    io = {n: nc.dram_tensor(f"in_{n}", a.shape, mybir.dt.from_np(a.dtype), kind="ExternalInput").ap()
          for n, a in arrays.items()}
    io["out"] = nc.dram_tensor("out_0", (B, T, C), F32, kind="ExternalOutput").ap()
    hybrid_kernel(nc, io, last_stage)


def kernel(**inputs):
    import concourse.bacc as _bacc
    from concourse.bass_utils import run_bass_kernel_spmd as _run

    arrays = device_inputs(inputs)
    nc = _bacc.Bacc("TRN2", target_bir_lowering=False, num_devices=1)
    program(nc, arrays)
    r = _run(nc, [{f"in_{n}": a for n, a in arrays.items()}], core_ids=[0])
    return r.results[0]["out_0"]
```

```python
from contextlib import ExitStack

import numpy as np

import concourse.bass as bass
from concourse import mybir

F32 = mybir.dt.float32
BF16 = mybir.dt.bfloat16
ALU = mybir.AluOpType
ACT = mybir.ActivationFunctionType
AX = mybir.AxisListType.X
ds = bass.ds

P = 128
B, T, C, H = 2, 2048, 256, 16
HD = C // H
KC = C // P
NT = T // P
CH = 4
NCH = NT // CH
NTT = B * NT
CW = CH * P
NE = 8
BH = B * H
CHUNK_STEPS = 3
LN_EPS = 1e-5
MASKED = -1e30
BANK = 512

A_TERMS = [(0, 0), (0, 1), (0, 2), (1, 0), (1, 1), (2, 0)]
A_D = 4
A_ROWS = A_D * len(A_TERMS)
A_K = A_ROWS + 3
LAG = 3
TURN_OUT_AT, TURN_MAX_AT = 2, 6
NORMALISE_AT = 14
CLIP = 1.0 - 1e-7
POWER = -3.2
PAIRS = NT // 2
AHEAD = 6
PSC = 3
ONE8, TWO8 = 0x38, 0x40


class Linked:

    def __init__(self, eng, sem, base=0):
        self.eng, self.sem, self.base, self.n = eng, sem, base, 0

    def __call__(self, ins):
        self.n += 1
        ins.then_inc(self.sem, 1)
        self.eng.wait_ge(self.sem, self.base + self.n)


def hybrid_kernel(nc, io):
    with ExitStack() as whole:
        def sb(name, shape, dt=F32, ctx=whole):
            return ctx.enter_context(nc.sbuf_tensor(name, shape, dt))

        def ps(name, shape, dt=F32, ctx=whole):
            return ctx.enter_context(nc.psum_tensor(name, shape, dt))

        VO = sb("VO", [P, BH, NT, HD])
        MEAN = sb("MEAN", [P, NTT])
        RS = sb("RS", [P, NTT])
        identf = sb("identf", [P, P])
        x_place = ExitStack()

        def place_x(name):
            return sb(name, [P, NTT, C], ctx=x_place)

        X = place_x("X")
        VO_tiles = VO[:].rearrange("p (b h) t d -> p b h t d", b=B)
        parts_a = {s: nc.dram_tensor(f"parts_a_{s}", [BH, len(A_TERMS), A_D, T], BF16).ap() for s in "qk"}
        parts_b = {s: nc.dram_tensor(f"parts_b_{s}", [BH, 3, HD, T], BF16).ap() for s in "qk"}

        x_kept = nc.dram_tensor("x_kept", [B, T, C], F32).ap()

        def stats_scratch(name, ctx):
            return (sb(name + "_moments", [P, CH, 6], ctx=ctx), sb(name + "_meanvar", [P, CH, 2], ctx=ctx),
                    sb(name + "_wait_word", [P, 1], ctx=ctx))

        def chunk_stats(link, n, scratch):
            moments, meanvar, word = scratch
            nc.vector.memset(word[:], 0.0)
            for t in range(CH):
                last = nc.vector.bn_stats(moments[:, t, :], X[:, ds(n * CH + t, 1), :].rearrange("p a n -> p (a n)"))
            link(last)
            nc.vector.memset(word[:], 0.0)
            for t in range(CH):
                last = nc.vector.bn_aggr(meanvar[:, t, :], moments[:, t, :])
            link(last)
            nc.vector.tensor_scalar(MEAN[:, ds(n * CH, CH)], meanvar[:, :, 0], 1.0, None, ALU.mult)
            link(nc.vector.tensor_scalar(RS[:, ds(n * CH, CH)], meanvar[:, :, 1], LN_EPS, None, ALU.add))

        def normalise_tile(out, tile):
            return nc.vector.tensor_scalar(out, X[:, ds(tile, 1), :].rearrange("p a n -> p (a n)"),
                                           MEAN[:, ds(tile, 1)], RS[:, ds(tile, 1)], ALU.subtract, ALU.mult)

        def rstd_stage(name):
            with ExitStack() as ctx:
                rooted = ctx.enter_context(nc.semaphore(name + "_rooted"))
                with nc.Block() as block:
                    @block.scalar
                    def _(act):
                        nc.scalar.activation(RS[:], RS[:], ACT.Sqrt).then_inc(rooted, 1)

                    @block.vector
                    def _(dve):
                        dve.wait_ge(rooted, 1)
                        nc.vector.reciprocal(RS[:], RS[:])

        def load_stage():
            with ExitStack() as ctx:
                st = stats_scratch("ld", ctx)
                x_in = ctx.enter_context(nc.semaphore("x_in"))
                consts_in = ctx.enter_context(nc.semaphore("consts_in"))
                steps = ctx.enter_context(nc.semaphore("ld_steps"))
                second_in = ctx.enter_context(nc.semaphore("second_in"))
                with nc.Block() as block:
                    @block.sync
                    def _(sp):
                        for b in range(B):
                            sp.dma_start(X[:, b * NT:(b + 1) * NT, :],
                                         io["x"][b].rearrange("(t p) c -> p t c", p=P)).then_inc(x_in if b == 0 else second_in, 16)
                        sp.dma_start(identf[:], io["ident"]).then_inc(consts_in, 16)
                        sp.wait_ge(consts_in, 16)

                    @block.vector
                    def _(dve):
                        for b, batch_in in enumerate((x_in, second_in)):
                            dve.wait_ge(batch_in, 16)
                            with dve.Fori(b * NCH, (b + 1) * NCH) as c:
                                chunk_stats(Linked(dve, steps, c * CHUNK_STEPS), c, st)

        def project_a_stage():
            with ExitStack() as ctx:
                def sem(name):
                    return ctx.enter_context(nc.semaphore("pa_" + name))

                wqk = sb("pa_wqk", [P, KC, 112], ctx=ctx)
                wv = sb("pa_wv", [P, KC, C], ctx=ctx)
                spread = sb("pa_spread", [112, P], ctx=ctx)
                qscale = sb("pa_qscale", [P, 1], ctx=ctx)
                xn = sb("pa_xn", [P, CH, C], ctx=ctx)
                xnT = [sb(f"pa_xnT{i}", [P, KC, CW], ctx=ctx) for i in range(2)]
                qk3 = sb("pa_qk3", [112, CW], ctx=ctx)
                z = sb("pa_z", [P, CW], ctx=ctx)
                rest = sb("pa_rest", [P, CW], ctx=ctx)
                part = [sb(f"pa_part{i}", [P, CW], BF16, ctx=ctx) for i in range(3)]
                psT = ps("pa_psT", [P, KC, CW], ctx=ctx)
                psV = ps("pa_psV", [P, CH, C], ctx=ctx)
                psQ = ps("pa_psQ", [P, CW], ctx=ctx)
                psZ = ps("pa_psZ", [P, CW], ctx=ctx)
                weights_in, normed, transposed, xnT_ready = sem("weights_in"), sem("normed"), sem("transposed"), sem("xnT_ready")
                v_ready, v_taken, q_ready, q_taken = sem("v_ready"), sem("v_taken"), sem("q_ready"), sem("q_taken")
                z_ready, z_taken, split, stored = sem("z_ready"), sem("z_taken"), sem("split"), sem("stored")
                with nc.Block() as block:
                    @block.sync
                    def _(sp):
                        sp.dma_start(wqk[:], io["wqk"].rearrange("(k p) n -> p k n", p=P)).then_inc(weights_in, 16)
                        sp.dma_start(wv[:], io["wv"].rearrange("(k p) n -> p k n", p=P)).then_inc(weights_in, 16)
                        sp.dma_start(spread[:], io["spread"]).then_inc(weights_in, 16)
                        sp.dma_start(qscale[:], io["qscale"]).then_inc(weights_in, 16)
                        n_store = 2 * len(A_TERMS)
                        with sp.Fori(0, B) as b:
                            with sp.Fori(0, NCH) as c:
                                sp.wait_ge(split, (b * NCH + c) * 3 + 3)
                                for s, half in (("q", 0), ("k", 1)):
                                    for j, terms in enumerate(A_TERMS):
                                        src = part[terms[half]][64 * half:64 * half + 64, :]
                                        dst = parts_a[s][ds(b * H, H), j, :, ds(c * CW, CW)]
                                        sp.dma_start(dst, src).then_inc(stored, 16)
                        sp.wait_ge(stored, B * NCH * n_store * 16)

                    @block.vector
                    def _(dve):
                        def normalise(n):
                            dve.wait_ge(transposed, n)
                            for t in range(CH):
                                normalise_tile(xn[:, t, :], n * CH + t).then_inc(normed, 1)

                        with dve.Fori(0, B) as b:
                            normalise(b * NCH)
                            for c in range(NCH):
                                n = b * NCH + c
                                if c + 1 < NCH:
                                    normalise(n + 1)
                                dve.wait_ge(q_ready, n + 1)
                                nc.vector.tensor_copy(qk3[:], psQ[0:112, :]).then_inc(q_taken, 1)
                                dve.wait_ge(v_ready, n + 1)
                                for t in range(CH):
                                    dst = VO_tiles[:, ds(b, 1), :, c * CH + t, :].rearrange("p a h d -> p (a h) d")
                                    nc.vector.tensor_copy(dst, psV[:, t, :].rearrange("p (h d) -> p h d", h=H)).then_inc(v_taken, 1)
                                dve.wait_ge(z_taken, n * 3 + 2)
                                nc.vector.tensor_tensor(rest[:], z[:], part[0][:], ALU.subtract).then_inc(split, 1)
                                dve.wait_ge(z_taken, n * 3 + 3)
                                nc.vector.tensor_tensor(part[2][:], rest[:], part[1][:], ALU.subtract).then_inc(split, 2)

                    @block.scalar
                    def _(act):
                        def copy_turned(n, par):
                            act.wait_ge(transposed, n + 1)
                            nc.scalar.activation(xnT[par][:], psT[:], ACT.Copy).then_inc(xnT_ready, 1)

                        act.wait_ge(weights_in, 64)
                        with act.Fori(0, B) as b:
                            act.wait_ge(v_ready, b * NCH)
                            copy_turned(b * NCH, 0)
                            for c in range(NCH):
                                n = b * NCH + c
                                if c + 1 < NCH:
                                    act.wait_ge(v_ready, n)
                                    copy_turned(n + 1, (c + 1) % 2)
                                act.wait_ge(z_ready, n + 1)
                                act.wait_ge(stored, n * (2 * len(A_TERMS) * 16))
                                nc.scalar.activation(z[:], psZ[:], ACT.Copy, scale=qscale[:]).then_inc(z_taken, 1)
                                act.wait_ge(z_taken, n * 3 + 1)
                                nc.scalar.activation(part[0][:], z[:], ACT.Copy).then_inc(z_taken, 1)
                                act.wait_ge(split, n * 3 + 1)
                                nc.scalar.activation(part[1][:], rest[:], ACT.Copy).then_inc(z_taken, 1)

                    @block.tensor
                    def _(pe):
                        def turn(n):
                            pe.wait_ge(xnT_ready, n)
                            for t in range(CH):
                                pe.wait_ge(normed, n * CH + (t + 1))
                                for k in range(KC):
                                    last = nc.tensor.transpose(psT[:, k, t * P:(t + 1) * P], xn[:, t, k * P:(k + 1) * P], identf[:])
                            last.then_inc(transposed, 1)

                        pe.wait_ge(weights_in, 64)
                        with pe.Fori(0, B) as b:
                            turn(b * NCH)
                            for c in range(NCH):
                                n, tokens = b * NCH + c, xnT[c % 2]
                                pe.wait_ge(xnT_ready, n + 1)
                                pe.wait_ge(q_taken, n)
                                for k in range(KC):
                                    last = nc.tensor.matmul(psQ[0:112, :], wqk[:, k, :], tokens[:, k, :], start=(k == 0), stop=(k == KC - 1))
                                last.then_inc(q_ready, 1)
                                if c + 1 < NCH:
                                    turn(n + 1)
                                pe.wait_ge(q_taken, n + 1)
                                pe.wait_ge(z_taken, n * 3)
                                nc.tensor.matmul(psZ[:], spread[:], qk3[:], start=True, stop=True).then_inc(z_ready, 1)
                                pe.wait_ge(v_taken, n * CH)
                                for t in range(CH):
                                    for k in range(KC):
                                        last = nc.tensor.matmul(psV[:, t, :], tokens[:, k, t * P:(t + 1) * P], wv[:, k, :],
                                                                start=(k == 0), stop=(k == KC - 1))
                                last.then_inc(v_ready, 1)

        def head_out(head):
            return VO[:, ds(head, 1), :, :].rearrange("p a (m j) d -> p (a m) j d", j=CH)

        def times_values(acc, strip, values, weights, first_tile, stop):
            m0 = max(0, -(-(first_tile - strip) // CH))
            if m0 >= CH:
                return None
            moving = weights.rearrange("p (m j n) -> p m j n", j=CH, n=P)[:, m0:, strip, :]
            return nc.tensor.matmul(acc[32 * strip:32 * strip + 32, m0 * P:BANK], values, moving,
                                    start=stop[0], stop=stop[1], skip_group_check=True)

        def attention_a_stage():
            units1 = [(i, c, min(c + BANK, (i + 1) * P)) for i in range(NT) for c in range(0, (i + 1) * P, BANK)]
            units2 = [(i, max(i * P, c), c + 2 * BANK) for i in range(NT) for c in range(0, T, 2 * BANK) if c + 2 * BANK > i * P]
            n1, n2 = len(units1), len(units2)
            pt_bufs = 4
            with ExitStack() as ctx:
                def sem(name):
                    return ctx.enter_context(nc.semaphore("aa_" + name))

                q1 = [sb(f"aa_q1_{i}", [P, T], BF16, ctx=ctx) for i in range(2)]
                k1 = [sb(f"aa_k1_{i}", [P, T], BF16, ctx=ctx) for i in range(2)]
                q2 = [sb(f"aa_q2_{i}", [P, T], BF16, ctx=ctx) for i in range(2)]
                k2 = [sb(f"aa_k2_{i}", [P, T], BF16, ctx=ctx) for i in range(2)]
                pt = [sb(f"aa_pt{i}", [P, T], ctx=ctx) for i in range(pt_bufs)]
                vst = [sb(f"aa_vst{i}", [P, NT, 32], ctx=ctx) for i in range(2)]
                masks = sb("aa_masks", [P, 2, P], ctx=ctx)
                maskb = sb("aa_maskb", [P, 2, P], BF16, ctx=ctx)
                identb = sb("aa_identb", [P, P], BF16, ctx=ctx)
                pmax = sb("aa_pmax", [P, CH, NT], ctx=ctx)
                negmax = sb("aa_negmax", [P, NT], ctx=ctx)
                mrest = sb("aa_mrest", [P, NT], ctx=ctx)
                mparts = sb("aa_mparts", [P, P], BF16, ctx=ctx)
                zeros = sb("aa_zeros", [P, NT], ctx=ctx)
                word = sb("aa_word", [P, 1], ctx=ctx)
                mrow = sb("aa_mrow", [3 * NT, P], BF16, ctx=ctx)
                u = sb("aa_u", [P, BANK], ctx=ctx)
                rsum = sb("aa_rsum", [P, CH, CH], ctx=ctx)
                ps1 = [ps(f"aa_ps1_{i}", [P, BANK], ctx=ctx) for i in range(2)]
                ps2 = [ps(f"aa_ps2_{i}", [P, 2 * BANK], ctx=ctx) for i in range(2)]
                acc = ps("aa_acc", [P, BANK], ctx=ctx)
                psT = ps("aa_psT", [P, CH, P], ctx=ctx)
                psM = psT[:, 0, :].bitcast(BF16)[:, 0:P]
                u_view = psT[:].rearrange("p m (j e) -> p m j e", j=CH)
                masks_in, cleared, consts = sem("masks_in"), sem("cleared"), sem("consts")
                cleared2 = sem("cleared2")
                in1, in2 = [sem("in1_0"), sem("in1_1")], [sem("in2_0"), sem("in2_1")]
                ready1, taken1 = sem("ready1"), sem("taken1")
                ready2, exped = sem("ready2"), sem("exped")
                pv_done = sem("pv_done")
                split = sem("split")
                m_turned, m_row, m_in = sem("m_turned"), sem("m_row"), sem("m_in")
                v_copied, acc_copied = sem("v_copied"), sem("acc_copied")
                u_turned, normalised = sem("u_turned"), sem("normalised")
                summed, max_steps, clear_steps = sem("summed"), sem("max_steps"), sem("clear_steps")
                max_links, split_links = CH, 5

                def all_steps(eng, step):
                    step(0, 0, 0)
                    step(1, 1, 0)
                    with eng.Fori(1, BH // 2 - 1) as k:
                        step(k * 2, 0, k)
                        step(k * 2 + 1, 1, k)
                    step(BH - 2, 0, BH // 2 - 1)
                    step(BH - 1, 1, BH // 2 - 1)

                def at_first(s):
                    return isinstance(s, int) and s == 0

                def has_head(s, n):
                    return not isinstance(s, int) or s + n < BH

                with nc.Block() as block:
                    @block.sync
                    def _(sp):
                        sp.dma_start(masks[:], io["masks"].rearrange("m p n -> p m n")).then_inc(masks_in, 16)
                        sp.wait_ge(cleared, 1)

                        def load(head, q, k, done):
                            for side, dst in (("q", q), ("k", k)):
                                src = parts_a[side][ds(head, 1)].rearrange("a e r t -> (a e r) t")
                                sp.dma_start(dst[0:A_ROWS, :], src).then_inc(done, 16)

                        def load_max(head, par):
                            sp.wait_ge(m_row, head + 1)
                            sp.dma_start(q2[par][A_ROWS:A_K, :].rearrange("a (t n) -> a t n", n=P), mrow[:]).then_inc(m_in, 16)

                        for g in range(2):
                            load(g, q1[g], k1[g], in1[g])
                        sp.wait_ge(cleared2, 2)
                        for g in range(2):
                            load(g, q2[g], k2[g], in2[g])
                        load_max(0, 0)
                        for g in range(2):
                            sp.wait_ge(ready1, n1 * (g + 1))
                            load(g + 2, q1[g], k1[g], in1[g])

                        def step(s, par, half):
                            if has_head(s, 1):
                                load_max(s + 1, 1 - par)
                            if has_head(s, 4):
                                sp.wait_ge(ready1, n1 * (s + 3))
                                load(s + 4, q1[par], k1[par], in1[par])
                            if has_head(s, 2):
                                sp.wait_ge(ready2, n2 * (s + 1))
                                load(s + 2, q2[par], k2[par], in2[par])

                        with sp.Fori(0, BH // 2 - 2) as k:
                            step(k * 2, 0, k)
                            step(k * 2 + 1, 1, k)
                        for s in range(BH - 4, BH):
                            step(s, s % 2, s // 2)

                    @block.vector
                    def _(dve):
                        link = Linked(dve, clear_steps)
                        for stack in q1 + k1:
                            nc.vector.memset(stack[:].bitcast(mybir.dt.uint32), 0)
                        for v in vst:
                            link(nc.vector.memset(v[:], 0.0))
                            nc.vector.memset(v[:, :, HD], 1.0)
                        nc.vector.memset(mparts[:].bitcast(mybir.dt.uint32), 0)
                        nc.vector.memset(zeros[:], 0.0)
                        nc.vector.memset(rsum[:], 0.0).then_inc(cleared, 1)
                        dve.wait_ge(masks_in, 16)
                        nc.vector.tensor_copy(maskb[:], masks[:])
                        nc.vector.tensor_copy(identb[:], identf[:]).then_inc(consts, 1)

                        def normalise(head):
                            dve.wait_ge(u_turned, head + 1)
                            nc.vector.reciprocal(rsum[:], u_view[:, :, :, HD]).then_inc(summed, 1)
                            dve.wait_ge(summed, head + 1)
                            nc.vector.tensor_tensor(head_out(head), u_view[:, :, :, 0:HD],
                                                    rsum[:].unsqueeze(3).broadcast_to([P, CH, CH, HD]),
                                                    ALU.mult).then_inc(normalised, 1)

                        def maxima(head, before=None):
                            for n, (i, c0, c1) in enumerate(units1):
                                dve.wait_ge(ready1, head * n1 + (n + 1))
                                nc.vector.tensor_reduce(pmax[:, c0 // BANK, i:i + 1], ps1[n % 2][:, 0:c1 - c0], AX,
                                                        ALU.max).then_inc(taken1, 1)
                                if n == NORMALISE_AT and before is not None:
                                    normalise(before)
                            dve.wait_ge(taken1, head * n1 + n1)
                            steps = Linked(dve, max_steps, head * max_links)
                            for c in range(1, CH):
                                steps(nc.vector.tensor_tensor(pmax[:, 0, CH * c:], pmax[:, 0, CH * c:], pmax[:, c, CH * c:], ALU.max))
                            dve.wait_ge(split, head * split_links)
                            steps(nc.vector.tensor_scalar(negmax[:], pmax[:, 0, :], -1.0, None, ALU.mult))

                        maxima(0)
                        maxima(1)

                        def step(s, par, half):
                            before = None if at_first(s) else s - 1
                            if has_head(s, 2):
                                maxima(s + 2, before)
                            else:
                                normalise(before)

                        all_steps(dve, step)
                        normalise(BH - 1)

                    @block.gpsimd
                    def _(pool):
                        for stack in q2 + k2:
                            last = nc.gpsimd.memset(stack[:].bitcast(mybir.dt.uint32), 0)
                        last.then_inc(cleared2, 1)
                        pool.wait_ge(cleared2, 1)
                        for stack in k2:
                            last = nc.gpsimd.memset(stack[0:A_K, :], 1.0)
                        last.then_inc(cleared2, 1)
                        pool.wait_ge(cleared, 1)

                        def copy_values(head, par):
                            src = VO[:, ds(head, 1), :, :].rearrange("p a t d -> p (a t) d")
                            nc.gpsimd.tensor_copy(vst[par][:, :, 0:HD], src).then_inc(v_copied, 1)

                        def split_max(head):
                            pool.wait_ge(max_steps, head * max_links + max_links)
                            pool.wait_ge(m_turned, head)
                            high, mid, low = (mparts[:, i * NT:(i + 1) * NT] for i in range(3))
                            steps = Linked(pool, split, head * split_links)
                            steps(nc.gpsimd.tensor_tensor(high, negmax[:], zeros[:], ALU.add))
                            steps(nc.gpsimd.tensor_tensor(mrest[:], negmax[:], high, ALU.subtract))
                            steps(nc.gpsimd.tensor_tensor(mid, mrest[:], zeros[:], ALU.add))
                            steps(nc.gpsimd.tensor_tensor(mrest[:], mrest[:], mid, ALU.subtract))
                            steps(nc.gpsimd.tensor_tensor(low, mrest[:], zeros[:], ALU.add))

                        copy_values(0, 0)
                        split_max(0)
                        split_max(1)

                        def step(s, par, half):
                            if has_head(s, 1):
                                if not at_first(s):
                                    pool.wait_ge(pv_done, s * NT)
                                    nc.gpsimd.tensor_tensor(word[:], zeros[:, 0:1], zeros[:, 0:1], ALU.add)
                                copy_values(s + 1, 1 - par)
                            if has_head(s, 2):
                                split_max(s + 2)

                        all_steps(pool, step)

                    @block.scalar
                    def _(act):
                        def copy_acc(head):
                            act.wait_ge(pv_done, head * NT + NT)
                            act.wait_ge(u_turned, head)
                            nc.scalar.activation(u[:], acc[:], ACT.Copy).then_inc(acc_copied, 1)

                        def copy_max_row(head):
                            act.wait_ge(m_turned, head + 1)
                            act.wait_ge(m_in, head * 16)
                            nc.scalar.activation(mrow[:], psM[0:3 * NT, :], ACT.Copy).then_inc(m_row, 1)

                        copy_max_row(0)

                        def step(s, par, half):
                            for n, (i, c0, c1) in enumerate(units2):
                                if i == 1 and units2[n - 1][0] == 0 and not at_first(s):
                                    copy_acc(s - 1)
                                if i == TURN_MAX_AT + 1 and units2[n - 1][0] == TURN_MAX_AT and has_head(s, 1):
                                    copy_max_row(s + 1)
                                act.wait_ge(ready2, s * n2 + (n + 1))
                                if not (at_first(s) and i < pt_bufs):
                                    act.wait_ge(pv_done, s * NT + (i + 1 - pt_bufs))
                                base = c1 - 2 * BANK
                                nc.scalar.activation(pt[i % pt_bufs][:, c0:c1], ps2[n % 2][:, c0 - base:c1 - base],
                                                     ACT.Exp).then_inc(exped, 1)

                        all_steps(act, step)
                        copy_acc(BH - 1)

                    @block.tensor
                    def _(pe):
                        pe.wait_ge(consts, 1)
                        last_unit = {i: n for n, (i, _, _) in enumerate(units2)}

                        def masked(out, lhsT, rhs, mask):
                            if mask is None:
                                return nc.tensor.matmul(out, lhsT, rhs, start=True, stop=True)
                            nc.tensor.matmul(out, lhsT, rhs, start=True, stop=False)
                            cols, m = mask
                            return nc.tensor.matmul(cols, identb[:], maskb[:, m, :], start=False, stop=True)

                        def scores1(head, par, n):
                            i, c0, c1 = units1[n]
                            if not (isinstance(head, int) and head == 0 and n < 2):
                                pe.wait_ge(taken1, head * n1 + (n - 1))
                            out = ps1[n % 2][:, 0:c1 - c0]
                            mask = (out[:, c1 - c0 - P:], 0) if c1 == (i + 1) * P else None
                            masked(out, q1[par][:, i * P:(i + 1) * P], k1[par][:, c0:c1], mask).then_inc(ready1, 1)

                        def scores2(head, par, n):
                            i, c0, c1 = units2[n]
                            if not (at_first(head) and n < 2):
                                pe.wait_ge(exped, head * n2 + (n - 1))
                            base = c1 - 2 * BANK
                            for b0 in range(base, c1, BANK):
                                a0 = max(b0, c0)
                                if a0 >= b0 + BANK:
                                    continue
                                out = ps2[n % 2][:, a0 - base:b0 + BANK - base]
                                mask = (out[:, 0:P], 1) if a0 == i * P else None
                                last = masked(out, k2[par][:, i * P:(i + 1) * P], q2[par][:, a0:b0 + BANK], mask)
                            last.then_inc(ready2, 1)

                        def product(head, par, i):
                            if i == 0:
                                pe.wait_ge(v_copied, head + 1)
                                pe.wait_ge(acc_copied, head)
                            pe.wait_ge(exped, head * n2 + (last_unit[i] + 1))
                            last = None
                            for j in range(CH):
                                mm = times_values(acc, j, vst[par][:, i, :], pt[i % pt_bufs][:], i, (i == 0, i == NT - CH + j))
                                last = mm or last
                            last.then_inc(pv_done, 1)
                            return last

                        def turn_out(head):
                            pe.wait_ge(acc_copied, head + 1)
                            for m in range(CH):
                                last = nc.tensor.transpose(psT[:, m, :], u[:, m * P:(m + 1) * P], identf[:])
                            last.then_inc(u_turned, 1)

                        def turn_max(head):
                            pe.wait_ge(split, head * split_links + split_links)
                            nc.tensor.transpose(psM, mparts[:], identb[:]).then_inc(m_turned, 1)

                        for g in range(2):
                            pe.wait_ge(in1[g], 32)
                            for n in range(n1):
                                scores1(g, g, n)
                        turn_max(0)

                        def step(s, par, half):
                            pe.wait_ge(in2[par], half * 32 + 32)
                            pe.wait_ge(m_in, s * 16 + 16)
                            n = columns = 0
                            for m, (i, c0, c1) in enumerate(units2):
                                columns += c1 - c0
                                share = n1 * columns // sum(b - a for _, a, b in units2) if has_head(s, 2) else 0
                                if m == 0 and has_head(s, 2):
                                    pe.wait_ge(in1[par], half * 32 + 64)
                                scores2(s, par, m)
                                while n < (n + share + 1) // 2:
                                    scores1(s + 2, par, n)
                                    n += 1
                                if m == last_unit[i]:
                                    if i >= LAG:
                                        product(s, par, i - LAG)
                                    if i == TURN_OUT_AT and not at_first(s):
                                        pe.wait_ge(m_row, s + 1)
                                        turn_out(s - 1)
                                    if i == TURN_MAX_AT and has_head(s, 1):
                                        if at_first(s):
                                            pe.wait_ge(m_row, 1)
                                        else:
                                            pe.wait_ge(normalised, s)
                                        turn_max(s + 1)
                                while n < share:
                                    scores1(s + 2, par, n)
                                    n += 1
                            for i in range(NT - LAG, NT):
                                product(s, par, i)

                        all_steps(pe, step)
                        pe.wait_ge(normalised, BH - 1)
                        turn_out(BH - 1)

        def out_project_stage(name, w_name, b_name, load_next, load_x=False):
            with ExitStack() as ctx:
                def sem(n):
                    return ctx.enter_context(nc.semaphore(f"{name}_{n}"))

                w = sb(f"{name}_w", [P, KC, C], ctx=ctx)
                bias = sb(f"{name}_bias", [P, C], ctx=ctx)
                gathered = [sb(f"{name}_gathered{i}", [P, CH, C], ctx=ctx) for i in range(2)]
                oT = [sb(f"{name}_oT{i}", [P, KC, CW], ctx=ctx) for i in range(2)]
                st = stats_scratch(name, ctx)
                psT = [ps(f"{name}_psT{i}", [P, KC, CW], ctx=ctx) for i in range(2)]
                psY = [ps(f"{name}_psY{i}", [P, CH, C], ctx=ctx) for i in range(2)]
                w_in, by_token, turned, oT_ready = sem("w_in"), sem("by_token"), sem("turned"), sem("oT_ready")
                y_ready, added, stat_steps, x_back = sem("y_ready"), sem("added"), sem("stat_steps"), sem("x_back")
                n_in = 16 + (16 if b_name else 0)

                def two_before(b, c):
                    return b * NCH + max(c - 1, 0)

                with nc.Block() as block:
                    @block.sync
                    def _(sp):
                        sp.dma_start(w[:], io[w_name].rearrange("(k p) n -> p k n", p=P)).then_inc(w_in, 16)
                        if b_name:
                            sp.dma_start(bias[:], io[b_name]).then_inc(w_in, 16)
                        if load_x:
                            for b in range(B):
                                sp.dma_start(X[:, b * NT:(b + 1) * NT, :], x_kept[b].rearrange("(t p) c -> p t c", p=P)).then_inc(x_back, 16)
                        load_next(sp)

                    @block.scalar
                    def _(act):
                        def gather(b, c):
                            act.wait_ge(turned, two_before(b, c))
                            for t in range(CH):
                                src = VO_tiles[:, ds(b, 1), :, c * CH + t, :].rearrange("p a h d -> p (a h) d")
                                last = nc.scalar.activation(gathered[c % 2][:, t, :].rearrange("p (h d) -> p h d", h=H), src, ACT.Copy)
                            last.then_inc(by_token, 1)

                        with act.Fori(0, B) as b:
                            for c in range(NCH):
                                gather(b, c)

                    @block.tensor
                    def _(pe):
                        def front(b, c):
                            n, par = b * NCH + c, c % 2
                            pe.wait_ge(oT_ready, two_before(b, c))
                            pe.wait_ge(by_token, n + 1)
                            for t in range(CH):
                                for k in range(KC):
                                    last = nc.tensor.transpose(psT[par][:, k, t * P:(t + 1) * P], gathered[par][:, t, k * P:(k + 1) * P], identf[:])
                            last.then_inc(turned, 1)

                        def back(b, c):
                            n, par = b * NCH + c, c % 2
                            pe.wait_ge(added, two_before(b, c))
                            pe.wait_ge(oT_ready, n + 1)
                            for t in range(CH):
                                for k in range(KC):
                                    last = nc.tensor.matmul(psY[par][:, t, :], oT[par][:, k, t * P:(t + 1) * P], w[:, k, :],
                                                            start=(k == 0), stop=(k == KC - 1))
                            last.then_inc(y_ready, 1)

                        pe.wait_ge(w_in, n_in)
                        with pe.Fori(0, B) as b:
                            front(b, 0)
                            for c in range(1, NCH):
                                front(b, c)
                                back(b, c - 1)
                            back(b, NCH - 1)

                    @block.vector
                    def _(dve):
                        def front(b, c):
                            n, par = b * NCH + c, c % 2
                            dve.wait_ge(y_ready, two_before(b, c))
                            dve.wait_ge(turned, n + 1)
                            nc.vector.tensor_copy(oT[par][:], psT[par][:]).then_inc(oT_ready, 1)

                        def back(b, c):
                            n = b * NCH + c
                            link = Linked(dve, stat_steps, n * (CHUNK_STEPS + (1 if b_name else 0)))
                            x_chunk = X[:, ds(n * CH, CH), :]
                            if b_name:
                                link(nc.vector.tensor_tensor(x_chunk, x_chunk, bias[:].unsqueeze(1).broadcast_to([P, CH, C]), ALU.add))
                            dve.wait_ge(y_ready, n + 1)
                            nc.vector.tensor_tensor(x_chunk, psY[c % 2][:], x_chunk, ALU.add).then_inc(added, 1)
                            dve.wait_ge(added, n + 1)
                            chunk_stats(link, n, st)

                        dve.wait_ge(w_in, n_in)
                        with dve.Fori(0, B) as b:
                            front(b, 0)
                            if load_x:
                                dve.wait_ge(x_back, B * 16)
                            for c in range(1, NCH):
                                front(b, c)
                                back(b, c - 1)
                            back(b, NCH - 1)

        def ffn_weights(name, ctx):
            ew = sb(f"{name}_ew", [P, KC, NE, C], ctx=ctx)
            eb = sb(f"{name}_eb", [NE, C], ctx=ctx)
            rw = sb(f"{name}_rw", [P, KC, NE], ctx=ctx)
            rb = sb(f"{name}_rb", [P, NE], ctx=ctx)
            countdown = sb(f"{name}_countdown", [P, NE], ctx=ctx)
            w_in = ctx.enter_context(nc.semaphore(f"{name}_w_in"))

            def load(sp):
                for k in range(KC):
                    sp.dma_start(ew[:, k, :, :], io["expert_w"][:, k * P:(k + 1) * P, :].rearrange("e p d -> p e d")).then_inc(w_in, 16)
                sp.dma_start(eb[:], io["expert_b"]).then_inc(w_in, 16)
                sp.dma_start(rw[:], io["router_w"].rearrange("(k p) n -> p k n", p=P)).then_inc(w_in, 16)
                sp.dma_start(rb[:], io["router_b"]).then_inc(w_in, 16)
                sp.dma_start(countdown[:], io["countdown"]).then_inc(w_in, 16)

            return (ew, eb, rw, rb, countdown, w_in), load

        def ffn_stage(name, weights):
            ew, eb, rw, rb, countdown, w_in = weights
            HALF = NE // 2
            with ExitStack() as ctx:
                def sem(n):
                    return ctx.enter_context(nc.semaphore(f"{name}_{n}"))

                xn = sb(f"{name}_xn", [P, CH, C], ctx=ctx)
                xnT = [sb(f"{name}_xnT{i}", [P, KC, CW], ctx=ctx) for i in range(2)]
                logit = sb(f"{name}_logit", [P, CH, NE], ctx=ctx)
                prob = sb(f"{name}_prob", [P, CH, NE], ctx=ctx)
                hit = sb(f"{name}_hit", [P, CH, NE], ctx=ctx)
                gate = sb(f"{name}_gate", [P, CH, NE], ctx=ctx)
                top = sb(f"{name}_top", [P, CH], ctx=ctx)
                total = sb(f"{name}_total", [P, CH], ctx=ctx)
                gateT = sb(f"{name}_gateT", [NE, CH, P], ctx=ctx)
                st = stats_scratch(name, ctx)
                psT = ps(f"{name}_psT", [P, KC, CW], ctx=ctx)
                psL = psT[:, 0, 0:CH * NE].rearrange("p (t e) -> p t e", e=NE)
                psG = psT[0:NE, 1, :].rearrange("p (t n) -> p t n", t=CH)
                psB = ps(f"{name}_psB", [P, CH, C], ctx=ctx)
                psE = [ps(f"{name}_psE{i}", [P, HALF, C], ctx=ctx) for i in range(2)]
                normed, turned, xnT_ready = sem("normed"), sem("turned"), sem("xnT_ready")
                logits_ready, shifted, exped = sem("logits_ready"), sem("shifted"), sem("exped")
                gated, gates_turned, gateT_ready = sem("gated"), sem("gates_turned"), sem("gateT_ready")
                bias_ready, e_ready = sem("bias_ready"), sem("e_ready")
                router_steps, x_steps = sem("router_steps"), sem("x_steps")
                n_chunks, units = B * NCH, 2 * CH
                router_links, x_links = 10, 1 + CH * NE + CHUNK_STEPS

                def used_at(u):
                    return HALF * (u % units + 1) + (1 if u % units >= 2 else 0) - (x_links if u < 0 else 0)

                def over_experts(ap):
                    return ap.unsqueeze(2).broadcast_to([P, CH, NE])

                def over_tokens(ap):
                    return ap.unsqueeze(1).broadcast_to([P, CH, NE])

                with nc.Block() as block:
                    @block.scalar
                    def _(act):
                        def copy_turned(n, par):
                            act.wait_ge(turned, n + 1)
                            nc.scalar.activation(xnT[par][:], psT[:], ACT.Copy).then_inc(xnT_ready, 1)

                        def chunk(n, par, more):
                            act.wait_ge(shifted, n + 1)
                            nc.scalar.activation(prob[:], logit[:], ACT.Exp).then_inc(exped, 1)
                            act.wait_ge(gates_turned, n + 1)
                            nc.scalar.activation(gateT[:], psG, ACT.Copy).then_inc(gateT_ready, 1)
                            if more:
                                copy_turned(n + 1, 1 - par)

                        copy_turned(0, 0)
                        with act.Fori(0, n_chunks // 2 - 1) as k:
                            for par in range(2):
                                chunk(k * 2 + par, par, True)
                        chunk(n_chunks - 2, 0, True)
                        chunk(n_chunks - 1, 1, False)

                    @block.tensor
                    def _(pe):
                        pe.wait_ge(w_in, 96)

                        def turn(n):
                            for t in range(CH):
                                pe.wait_ge(normed, n * CH + (t + 1))
                                for k in range(KC):
                                    last = nc.tensor.transpose(psT[:, k, t * P:(t + 1) * P], xn[:, t, k * P:(k + 1) * P], identf[:])
                            last.then_inc(turned, 1)

                        def expert_unit(n, par, u):
                            t, half = u // 2, u % 2
                            if not (isinstance(n, int) and n == 0 and u < 2):
                                pe.wait_ge(x_steps, n * x_links + used_at(u - 2))
                            for pair in range(0, HALF, 2):
                                for k in range(KC):
                                    e = half * HALF + pair
                                    last = nc.tensor.matmul(psE[u % 2][:, pair:pair + 2, :], xnT[par][:, k, t * P:(t + 1) * P],
                                                            ew[:, k, e:e + 2, :], start=(k == 0), stop=(k == KC - 1))
                            last.then_inc(e_ready, 1)

                        def chunk(n, par, more):
                            pe.wait_ge(xnT_ready, n + 1)
                            for t in range(CH):
                                for k in range(KC):
                                    last = nc.tensor.matmul(psL[:, t, :], xnT[par][:, k, t * P:(t + 1) * P], rw[:, k, :],
                                                            start=(k == 0), stop=(k == KC - 1))
                            last.then_inc(logits_ready, 1)
                            for u in range(2):
                                expert_unit(n, par, u)
                            pe.wait_ge(gated, n + 1)
                            for t in range(CH):
                                last = nc.tensor.transpose(psG[:, t, :], gate[:, t, :], identf[:])
                            last.then_inc(gates_turned, 1)
                            expert_unit(n, par, 2)
                            pe.wait_ge(gateT_ready, n + 1)
                            for t in range(CH):
                                last = nc.tensor.matmul(psB[:, t, :], gateT[:, t, :], eb[:], start=True, stop=True)
                            last.then_inc(bias_ready, 1)
                            for u in range(3, units):
                                if u == 5 and more:
                                    turn(n + 1)
                                expert_unit(n, par, u)

                        turn(0)
                        chunk(0, 0, True)
                        chunk(1, 1, True)
                        with pe.Fori(1, n_chunks // 2 - 1) as k:
                            for par in range(2):
                                chunk(k * 2 + par, par, True)
                        chunk(n_chunks - 2, 0, True)
                        chunk(n_chunks - 1, 1, False)

                    @block.vector
                    def _(dve):
                        dve.wait_ge(w_in, 96)

                        def normalise(n):
                            dve.wait_ge(turned, n)
                            for t in range(CH):
                                normalise_tile(xn[:, t, :], n * CH + t).then_inc(normed, 1)

                        def route(n):
                            link = Linked(dve, router_steps, n * router_links)
                            dve.wait_ge(logits_ready, n + 1)
                            link(nc.vector.tensor_tensor(logit[:], psL, over_tokens(rb[:]), ALU.add))
                            link(nc.vector.tensor_reduce(top[:], logit[:], AX, ALU.max))
                            nc.vector.tensor_tensor(logit[:], logit[:], over_experts(top[:]), ALU.subtract).then_inc(shifted, 1)
                            dve.wait_ge(exped, n + 1)
                            link(nc.vector.tensor_reduce(total[:], prob[:], AX, ALU.add))
                            link(nc.vector.reciprocal(total[:], total[:]))
                            link(nc.vector.tensor_tensor(prob[:], prob[:], over_experts(total[:]), ALU.mult))
                            link(nc.vector.tensor_reduce(top[:], prob[:], AX, ALU.max))
                            link(nc.vector.tensor_tensor(hit[:], prob[:], over_experts(top[:]), ALU.is_equal))
                            link(nc.vector.tensor_tensor(hit[:], hit[:], over_tokens(countdown[:]), ALU.mult))
                            link(nc.vector.tensor_reduce(top[:], hit[:], AX, ALU.max))
                            link(nc.vector.tensor_tensor(hit[:], hit[:], over_experts(top[:]), ALU.is_equal))
                            nc.vector.tensor_tensor(gate[:], hit[:], prob[:], ALU.mult).then_inc(gated, 1)
                            dve.wait_ge(gated, n + 1)

                        def chunk(n, more):
                            route(n)
                            link = Linked(dve, x_steps, n * x_links)
                            for u in range(units):
                                t, half = u // 2, u % 2
                                if u == 2:
                                    dve.wait_ge(bias_ready, n + 1)
                                    x_chunk = X[:, ds(n * CH, CH), :]
                                    link(nc.vector.tensor_tensor(x_chunk, psB[:], x_chunk, ALU.add))
                                dve.wait_ge(e_ready, n * units + (u + 1))
                                x_tile = X[:, ds(n * CH + t, 1), :].rearrange("p a n -> p (a n)")
                                for e in range(HALF):
                                    g = half * HALF + e
                                    link(nc.vector.scalar_tensor_tensor(x_tile, psE[u % 2][:, e, :], gate[:, t, g:g + 1],
                                                                        x_tile, ALU.mult, ALU.add))
                                if u == 3 and more:
                                    normalise(n + 1)
                            chunk_stats(link, n, st)

                        normalise(0)
                        with dve.Fori(0, n_chunks - 1) as n:
                            chunk(n, True)
                        chunk(n_chunks - 1, False)

        def project_b_stage():
            with ExitStack() as ctx:
                def sem(name):
                    return ctx.enter_context(nc.semaphore("pb_" + name))

                HB = 2 * C // P
                w = sb("pb_w", [P, KC, 3 * C], ctx=ctx)
                bias = sb("pb_bias", [P, 3 * C], ctx=ctx)
                xn = sb("pb_xn", [P, CH, C], ctx=ctx)
                xnT = sb("pb_xnT", [P, KC, CW], ctx=ctx)
                qk = [sb(f"pb_qk{i}", [P, CH, 2 * C], ctx=ctx) for i in range(2)]
                square = sb("pb_square", [P, CH, 2 * C], ctx=ctx)
                norm = sb("pb_norm", [P, CH * 2 * H], ctx=ctx)
                rest = sb("pb_rest", [P, HB, CW], ctx=ctx)
                part = [sb(f"pb_part{i}", [P, HB, CW], BF16, ctx=ctx) for i in range(3)]
                psT = ps("pb_psT", [P, KC, CW], ctx=ctx)
                psQK = [ps(f"pb_psQK{i}", [P, 2 * C], ctx=ctx) for i in range(2)]
                psR = ps("pb_psR", [P, HB, CW], ctx=ctx)
                psV = psT[:].rearrange("p k (t n) -> p (k t) n", n=C)
                w_in, normed, turned, xnT_ready = sem("w_in"), sem("normed"), sem("turned"), sem("xnT_ready")
                qk_ready, qk_taken, v_ready, v_taken = sem("qk_ready"), sem("qk_taken"), sem("v_ready"), sem("v_taken")
                squared, summed, rooted, norm_steps = sem("squared"), sem("summed"), sem("rooted"), sem("norm_steps")
                unit_ready, unit_turned, x_stored = sem("unit_ready"), sem("unit_turned"), sem("x_stored")
                high, rested, mid, rested2, low, stored = (sem(x) for x in ("high", "rested", "mid", "rested2", "low", "stored"))
                n_stores = 3 * HB

                def batches(eng, beside):
                    with eng.Fori(0, B) as b:
                        for c in range(NCH + 1):
                            beside(b, c if c < NCH else None, c - 1 if c > 0 else None)

                with nc.Block() as block:
                    @block.sync
                    def _(sp):
                        sp.dma_start(w[:], io["w_qkv"].rearrange("(k p) n -> p k n", p=P)).then_inc(w_in, 16)
                        sp.dma_start(bias[:], io["b_qkv"]).then_inc(w_in, 16)
                        for b in range(B):
                            sp.dma_start(x_kept[b].rearrange("(t p) c -> p t c", p=P), X[:, b * NT:(b + 1) * NT, :]).then_inc(x_stored, 16)
                        with sp.Fori(0, B) as b:
                            with sp.Fori(0, NCH) as c:
                                n = b * NCH + c
                                for i, made in enumerate((high, mid, low)):
                                    sp.wait_ge(made, n + 1)
                                    for blk in range(HB):
                                        side, heads = "qk"[blk // 2], (blk % 2) * (H // 2)
                                        dst = parts_b[side][ds(b * H + heads, H // 2), i, :, ds(c * CW, CW)]
                                        sp.dma_start(dst, part[i][:, blk, :]).then_inc(stored, 16)
                        sp.wait_ge(stored, B * NCH * n_stores * 16)
                        sp.wait_ge(x_stored, B * 16)

                    @block.scalar
                    def _(act):
                        def beside(b, front, back):
                            if front is not None:
                                n = b * NCH + front
                                act.wait_ge(turned, n + 1)
                                nc.scalar.activation(xnT[:], psT[:], ACT.Copy).then_inc(xnT_ready, 1)
                            if back is not None:
                                m = b * NCH + back
                                act.wait_ge(summed, m + 1)
                                nc.scalar.activation(norm[:], norm[:], ACT.Sqrt).then_inc(rooted, 1)
                                act.wait_ge(unit_turned, m + 1)
                                act.wait_ge(stored, m * (n_stores * 16))
                                nc.scalar.activation(part[0][:], psR[:], ACT.Copy).then_inc(high, 1)
                            if front is not None:
                                act.wait_ge(qk_taken, n * CH + CH)
                                act.wait_ge(summed, n)
                                nc.scalar.activation(square[:], qk[front % 2][:], ACT.Square).then_inc(squared, 1)
                            if back is not None:
                                act.wait_ge(rested, m + 1)
                                nc.scalar.activation(part[1][:], rest[:], ACT.Copy).then_inc(mid, 1)

                        batches(act, beside)

                    @block.gpsimd
                    def _(pool):
                        with pool.Fori(0, B * NCH) as n:
                            pool.wait_ge(mid, n + 1)
                            nc.gpsimd.tensor_tensor(part[2][:], rest[:], part[1][:], ALU.subtract).then_inc(low, 1)

                    @block.tensor
                    def _(pe):
                        pe.wait_ge(w_in, 32)

                        def beside(b, front, back):
                            if front is not None:
                                n = b * NCH + front
                                pe.wait_ge(v_taken, n * CH)
                                for t in range(CH):
                                    pe.wait_ge(normed, n * CH + (t + 1))
                                    for k in range(KC):
                                        last = nc.tensor.transpose(psT[:, k, t * P:(t + 1) * P], xn[:, t, k * P:(k + 1) * P], identf[:])
                                last.then_inc(turned, 1)
                                pe.wait_ge(xnT_ready, n + 1)
                                for t in range(CH):
                                    pe.wait_ge(qk_taken, n * CH + max(t - 1, 0))
                                    for k in range(KC):
                                        last = nc.tensor.matmul(psQK[t % 2][:], xnT[:, k, t * P:(t + 1) * P], w[:, k, 0:2 * C],
                                                                start=(k == 0), stop=(k == KC - 1))
                                    last.then_inc(qk_ready, 1)
                                    if t == 1 and back is not None:
                                        turn_units(b * NCH + back, back % 2)
                                for t in range(CH):
                                    for k in range(KC):
                                        last = nc.tensor.matmul(psV[:, t, :], xnT[:, k, t * P:(t + 1) * P], w[:, k, 2 * C:3 * C],
                                                                start=(k == 0), stop=(k == KC - 1))
                                last.then_inc(v_ready, 1)
                            else:
                                turn_units(b * NCH + back, back % 2)

                        def turn_units(n, par):
                            pe.wait_ge(unit_ready, n + 1)
                            pe.wait_ge(rested, n)
                            for blk in range(HB):
                                for t in range(CH):
                                    last = nc.tensor.transpose(psR[:, blk, t * P:(t + 1) * P], qk[par][:, t, blk * P:(blk + 1) * P], identf[:])
                            last.then_inc(unit_turned, 1)

                        batches(pe, beside)

                    @block.vector
                    def _(dve):
                        dve.wait_ge(w_in, 32)
                        def beside(b, front, back):
                            if front is not None:
                                n = b * NCH + front
                                dve.wait_ge(turned, n)
                                for t in range(CH):
                                    normalise_tile(xn[:, t, :], n * CH + t).then_inc(normed, 1)
                            if back is not None:
                                m = b * NCH + back
                                unit_vectors(m, qk[back % 2])
                            if front is not None:
                                dve.wait_ge(unit_turned, b * NCH + (front - 1 if front > 0 else 0))
                                for t in range(CH):
                                    dve.wait_ge(qk_ready, n * CH + (t + 1))
                                    nc.vector.tensor_tensor(qk[front % 2][:, t, :], psQK[t % 2][:], bias[:, 0:2 * C], ALU.add).then_inc(qk_taken, 1)
                            if back is not None:
                                dve.wait_ge(high, m + 1)
                                dve.wait_ge(low, m)
                                nc.vector.tensor_tensor(rest[:], psR[:], part[0][:], ALU.subtract).then_inc(rested, 1)
                            if front is not None:
                                dve.wait_ge(v_ready, n + 1)
                                for t in range(CH):
                                    dst = VO_tiles[:, ds(b, 1), :, front * CH + t, :].rearrange("p a h d -> p (a h) d")
                                    nc.vector.tensor_tensor(dst, psV[:, t, :].rearrange("p (h d) -> p h d", h=H),
                                                            bias[:, 2 * C:].rearrange("p (h d) -> p h d", h=H), ALU.add).then_inc(v_taken, 1)

                        def unit_vectors(n, qk):
                            link = Linked(dve, norm_steps, n * 2)
                            dve.wait_ge(squared, n + 1)
                            dve.wait_ge(unit_ready, n)
                            nc.vector.tensor_reduce(norm[:], square[:].rearrange("p t (h d) -> p (t h) d", d=HD), AX, ALU.add).then_inc(summed, 1)
                            dve.wait_ge(rooted, n + 1)
                            link(nc.vector.tensor_scalar(norm[:], norm[:], 1e-12, None, ALU.max))
                            link(nc.vector.reciprocal(norm[:], norm[:]))
                            qk_heads = qk[:].rearrange("p t (h d) -> p (t h) d", d=HD)
                            nc.vector.tensor_tensor(qk_heads, qk_heads, norm[:].unsqueeze(2).broadcast_to([P, CH * 2 * H, HD]),
                                                    ALU.mult).then_inc(unit_ready, 1)

                        batches(dve, beside)

        def attention_b_stage():
            UNIT = 2 * BANK
            per_tile, per_pair = T // UNIT, 2 * T // UNIT
            n_units = NT * per_tile
            q_runs = [(0, 3), (1, 2), (2, 1)]
            k_runs = [3, 2, 1]
            K1 = HD * sum(terms for _, terms in q_runs)
            K2 = K1 + 1
            with ExitStack() as ctx:
                def sem(name):
                    return ctx.enter_context(nc.semaphore("ab_" + name))

                f = sb("ab_f", [P, NT, T], ctx=ctx)
                qs = sb("ab_qs", [P, T], BF16, ctx=ctx)
                ks = sb("ab_ks", [P, T], BF16, ctx=ctx)
                neg = sb("ab_neg", [P, NT, T], mybir.dt.uint8, ctx=ctx)
                two = sb("ab_two", [P, P], mybir.dt.uint8, ctx=ctx)
                ncol = sb("ab_ncol", [P, NT], ctx=ctx)
                rcol = sb("ab_rcol", [P, NT], ctx=ctx)
                vst = sb("ab_vst", [P, NT, 32], ctx=ctx)
                u = sb("ab_u", [P, BANK], ctx=ctx)
                least = sb("ab_least", [P, CH, CH], ctx=ctx)
                rsum = sb("ab_rsum", [P, CH, CH], ctx=ctx)
                psC = [ps(f"ab_psC{i}", [P, UNIT], ctx=ctx) for i in range(PSC)]
                acc = ps("ab_acc", [P, BANK], ctx=ctx)
                psT = ps("ab_psT", [P, CH, P], ctx=ctx)
                u_view = psT[:].rearrange("p m (j e) -> p m j e", j=CH)
                two8 = two[:].bitcast(mybir.dt.float8e4)
                neg8 = neg[:].bitcast(mybir.dt.float8e4)
                cleared, stacks_in = sem("cleared"), sem("stacks_in")
                c_ready, c_taken = sem("c_ready"), sem("c_taken")
                squared = sem("squared")
                rooted, arctaned, logged = sem("rooted"), sem("arctaned"), sem("logged")
                neg_ready, halved = sem("neg_ready"), sem("halved")
                f_ready = sem("f_ready")
                scale_steps, scaled, pv_done = sem("scale_steps"), sem("scaled"), sem("pv_done")
                acc_copied, u_turned, out_steps = sem("acc_copied"), sem("u_turned"), sem("out_steps")
                n_loads, out_links = 16 * (len(q_runs) + len(k_runs)), 4

                def head_units(head):
                    return head * (2 * n_units)

                def all_heads(eng, step):
                    with eng.Fori(0, BH - 1) as h:
                        step(h, True)
                    step(BH - 1, False)

                with nc.Block() as block:
                    @block.sync
                    def _(sp):
                        def load(head):
                            row = 0
                            for part, terms in q_runs:
                                src = parts_b["q"][ds(head, 1), part].broadcast_to([terms, HD, T])
                                sp.dma_start(qs[row:row + terms * HD, :],
                                             src).then_inc(stacks_in, 16)
                                row += terms * HD
                            row = 0
                            for terms in k_runs:
                                src = parts_b["k"][ds(head, 1), 0:terms].rearrange("a e d t -> (a e d) t")
                                sp.dma_start(ks[row:row + terms * HD, :], src).then_inc(stacks_in, 16)
                                row += terms * HD

                        sp.wait_ge(cleared, 2)
                        load(0)
                        with sp.Fori(0, BH - 1) as h:
                            sp.wait_ge(c_ready, head_units(h + 1))
                            load(h + 1)

                    @block.tensor
                    def _(pe):
                        def unit(head, second, n):
                            at = second * n_units + n
                            before = n - PSC if n >= PSC else max(m for m in range(n_units) if m % PSC == n) - n_units
                            if not (isinstance(head, int) and head == 0 and at + before - n < 0):
                                pe.wait_ge(c_taken, head_units(head) + (at + before - n + 1))
                            i, half = n // per_tile, n % per_tile
                            rows = K2 if second else K1
                            if second and n % per_pair == 0:
                                pe.wait_ge(neg_ready, head * PAIRS + (n // per_pair + 1))
                            for c in range(0, UNIT, BANK):
                                q0 = half * UNIT + c
                                last = nc.tensor.matmul(psC[n % PSC][:, c:c + BANK], ks[0:rows, i * P:(i + 1) * P], qs[0:rows, q0:q0 + BANK],
                                                        start=True, stop=not second)
                            for c in range(0, UNIT if second else 0, BANK):
                                q0 = half * UNIT + c
                                last = nc.tensor.matmul(psC[n % PSC][:, c:c + BANK], two8, neg8[:, i, q0:q0 + BANK],
                                                        start=False, stop=True)
                            last.then_inc(c_ready, 1)

                        def first_units(head, p, some=range(per_pair)):
                            if p == 0:
                                pe.wait_ge(stacks_in, head * n_loads + n_loads)
                            for m in some:
                                unit(head, 0, p * per_pair + m)

                        def product(head, i):
                            if i == 0:
                                pe.wait_ge(acc_copied, head)
                            if i % 2 == 0:
                                pe.wait_ge(scaled, head * PAIRS + (i // 2 + 1))
                            for j in range(CH):
                                last = times_values(acc, j, vst[:, i, :], f[:, i, :], 0, (i == 0, i == NT - 1))
                            if i % 2 == 1:
                                last.then_inc(pv_done, 1)

                        def step(head, has_next):
                            for n in range(n_units):
                                unit(head, 1, n)
                            for p in range(PAIRS):
                                if has_next and p > 0:
                                    first_units(head + 1, p - 1, range(PSC))
                                product(head, 2 * p)
                                if has_next and p > 0:
                                    first_units(head + 1, p - 1, range(PSC, per_pair))
                                product(head, 2 * p + 1)
                            if has_next:
                                first_units(head + 1, PAIRS - 1)
                            pe.wait_ge(acc_copied, head + 1)
                            pe.wait_ge(out_steps, head * out_links)
                            for m in range(CH):
                                last = nc.tensor.transpose(psT[:, m, :], u[:, m * P:(m + 1) * P], identf[:])
                            last.then_inc(u_turned, 1)

                        for p in range(PAIRS):
                            first_units(0, p)
                        all_heads(pe, step)

                    @block.vector
                    def _(dve):
                        nc.vector.memset(vst[:], 0.0).then_inc(cleared, 1)
                        dve.wait_ge(cleared, 1)
                        nc.vector.memset(vst[:, :, HD + 1], 1.0)
                        nc.vector.memset(ks[K1:K1 + 32, :], -1.0)
                        nc.vector.memset(qs[K1:K1 + 32, :], 1.0)
                        nc.vector.tensor_scalar(two[:], identf[:], TWO8, None, ALU.mult).then_inc(cleared, 1)

                        def clip_pair(head, p):
                            for m in range(per_pair):
                                n = p * per_pair + m
                                i, q0 = n // per_tile, n % per_tile * UNIT
                                dve.wait_ge(c_ready, head_units(head) + (n + 1))
                                nc.vector.tensor_scalar(f[:, i, q0:q0 + UNIT], psC[n % PSC][:], CLIP, -CLIP,
                                                        ALU.min, ALU.max).then_inc(c_taken, 1)
                            dve.wait_ge(c_taken, head_units(head) + (p + 1) * per_pair)
                            pair = f[:, 2 * p:2 * p + 2, :]
                            nc.vector.tensor_scalar(neg[:, 2 * p:2 * p + 2, :], pair, 0.0, ONE8, ALU.is_lt, ALU.mult).then_inc(neg_ready, 1)

                        def tangent_pair(head, p):
                            dve.wait_ge(rooted, head * PAIRS + (p + 1))
                            for n in range(p * per_pair, (p + 1) * per_pair):
                                i, q0 = n // per_tile, n % per_tile * UNIT
                                dve.wait_ge(c_ready, head_units(head) + (n_units + n + 1))
                                place = f[:, i, q0:q0 + UNIT]
                                nc.vector.tensor_tensor(place, psC[n % PSC][:], place, ALU.mult).then_inc(c_taken, 1)

                        def half_angle(head, p):
                            dve.wait_ge(arctaned, head * PAIRS + (p + 1))
                            pair = f[:, 2 * p:2 * p + 2, :]
                            nc.vector.scalar_tensor_tensor(pair, neg[:, 2 * p:2 * p + 2, :], float(np.pi) / 2 / ONE8, pair,
                                                           ALU.mult, ALU.subtract).then_inc(halved, 1)

                        def scale_values(head, p):
                            two = slice(2 * p, 2 * p + 2)
                            dve.wait_ge(f_ready, head * NT + (2 * p + 2))
                            nc.vector.reciprocal(rcol[:, two], ncol[:, two]).then_inc(scale_steps, 1)
                            dve.wait_ge(scale_steps, head * PAIRS + (p + 1))
                            nc.vector.tensor_copy(vst[:, two, HD], rcol[:, two])
                            values = VO[:, ds(head, 1), two, :].rearrange("p a t d -> p (a t) d")
                            nc.vector.tensor_tensor(vst[:, two, 0:HD], values, rcol[:, two].unsqueeze(2).broadcast_to([P, 2, HD]),
                                                    ALU.mult).then_inc(scaled, 1)

                        def step(head, has_next):
                            for p in range(PAIRS):
                                tangent_pair(head, p)
                            for p in range(AHEAD):
                                half_angle(head, p)
                            for p in range(PAIRS):
                                if p + AHEAD < PAIRS:
                                    half_angle(head, p + AHEAD)
                                scale_values(head, p)
                                if has_next and p > 0:
                                    dve.wait_ge(pv_done, head * PAIRS + p)
                                    clip_pair(head + 1, p - 1)
                            dve.wait_ge(pv_done, head * PAIRS + PAIRS)
                            dve.wait_ge(u_turned, head)
                            nc.vector.tensor_copy(u[:], acc[:]).then_inc(acc_copied, 1)
                            if has_next:
                                clip_pair(head + 1, PAIRS - 1)
                            link = Linked(dve, out_steps, head * out_links)
                            dve.wait_ge(u_turned, head + 1)
                            link(nc.vector.tensor_scalar(least[:], u_view[:, :, :, HD + 1], 1e-12, None, ALU.mult))
                            link(nc.vector.tensor_tensor(rsum[:], u_view[:, :, :, HD], least[:], ALU.max))
                            link(nc.vector.reciprocal(rsum[:], rsum[:]))
                            link(nc.vector.tensor_tensor(head_out(head), u_view[:, :, :, 0:HD],
                                                         rsum[:].unsqueeze(3).broadcast_to([P, CH, CH, HD]), ALU.mult))

                        for p in range(PAIRS):
                            clip_pair(0, p)
                        all_heads(dve, step)

                    @block.gpsimd
                    def _(pool):
                        with pool.Fori(0, BH) as h:
                            for p in range(PAIRS):
                                pool.wait_ge(neg_ready, h * PAIRS + (p + 1))
                                pair = f[:, 2 * p:2 * p + 2, :].rearrange("p a t -> p (a t)")
                                nc.gpsimd.tensor_tensor(pair, pair, pair, ALU.mult).then_inc(squared, 1)

                    @block.scalar
                    def _(act):
                        def pair_of(p):
                            return f[:, 2 * p:2 * p + 2, :].rearrange("p a t -> p (a t)")

                        with act.Fori(0, BH) as h:
                            for p in range(PAIRS):
                                act.wait_ge(squared, h * PAIRS + (p + 1))
                                nc.scalar.activation(pair_of(p), pair_of(p), ACT.Abs_reciprocal_sqrt, bias=1.0, scale=-1.0).then_inc(rooted, 1)
                            for p in range(PAIRS):
                                act.wait_ge(c_taken, head_units(h) + (n_units + (p + 1) * per_pair))
                                nc.scalar.activation(pair_of(p), pair_of(p), ACT.Arctan).then_inc(arctaned, 1)
                            nc.scalar.preload_act_table_set("natural_log_exp_and_others")

                            def log_pair(p):
                                act.wait_ge(halved, h * PAIRS + (p + 1))
                                nc.scalar.activation(pair_of(p), pair_of(p), ACT.Ln, bias=1.0, scale=2.0).then_inc(logged, 1)

                            log_pair(0)
                            for p in range(PAIRS):
                                if p + 1 < PAIRS:
                                    log_pair(p + 1)
                                act.wait_ge(logged, h * PAIRS + (p + 1))
                                for i in (2 * p, 2 * p + 1):
                                    nc.scalar.activation(f[:, i, :], f[:, i, :], ACT.Exp, scale=POWER,
                                                         accum_out=ncol[:, i:i + 1]).then_inc(f_ready, 1)

        def out_project_and_ffn(out_name, w_name, b_name, ln_name, ffn_name, load_x=False):
            with ExitStack() as ctx:
                weights, load = ffn_weights(ffn_name, ctx)
                out_project_stage(out_name, w_name, b_name, load, load_x)
                rstd_stage(ln_name)
                ffn_stage(ffn_name, weights)

        load_stage()
        rstd_stage("ln1")
        project_a_stage()
        attention_a_stage()
        out_project_and_ffn("oa", "wo", None, "ln2", "f1")
        rstd_stage("ln3")
        project_b_stage()
        x_place.close()
        attention_b_stage()
        X = place_x("X_again")
        out_project_and_ffn("ob", "w_out", "b_out", "ln4", "f2", load_x=True)
        with ExitStack() as ctx:
            out_done = ctx.enter_context(nc.semaphore("out_done"))
            with nc.Block() as block:
                @block.sync
                def _(sp):
                    for b in range(B):
                        sp.dma_start(io["out"][b].rearrange("(t p) c -> p t c", p=P),
                                     X[:, b * NT:(b + 1) * NT, :]).then_inc(out_done, 16)
                    sp.wait_ge(out_done, 16 * B)
        x_place.close()


def device_inputs(inputs):
    g = {k: np.asarray(v) for k, v in inputs.items()}
    f = np.float32
    wq, wk = g["L0_attn_a_wq"], g["L0_attn_a_wk"]
    wqk = np.zeros((C, 112), f)
    wqk[:, 0:48], wqk[:, 64:112] = wq, wk
    spread = np.zeros((112, P), f)
    for half in (0, 64):
        for h in range(H):
            for d in range(3):
                spread[half + 3 * h + d, half + A_D * h + d] = 1.0
                spread[half + 3 * h + d, half + A_D * h + 3] = g["L0_attn_a_head_dirs"][h, d]
    qscale = np.ones((P, 1), f)
    for h in range(H):
        qscale[A_D * h:A_D * h + 3, 0] = g["L0_attn_a_scale"][0]
    row, col = np.indices((P, P))
    upper = np.where(col > row, MASKED, 0.0).astype(f)
    lower = np.where(row > col, MASKED, 0.0).astype(f)
    spread_over = lambda a: np.ascontiguousarray(np.broadcast_to(a, (P, a.size)))
    return {
        "x": g["L0_attn_a_x"], "wqk": wqk, "wv": g["L0_attn_a_wv"], "wo": g["L0_attn_a_wo"],
        "spread": spread, "qscale": qscale, "ident": np.eye(P, dtype=f), "masks": np.stack([upper, lower]),
        "w_qkv": np.ascontiguousarray(g["L0_attn_b_w_qkv"].T), "b_qkv": spread_over(g["L0_attn_b_b_qkv"]),
        "w_out": np.ascontiguousarray(g["L0_attn_b_w_out"].T), "b_out": spread_over(g["L0_attn_b_b_out"]),
        "router_w": g["L0_ffn_router_w"], "router_b": spread_over(g["L0_ffn_router_b"]),
        "countdown": spread_over(np.arange(NE, 0, -1).astype(f)),
        "expert_w": g["L0_ffn_expert_w"], "expert_b": g["L0_ffn_expert_b"],
    }


def program(nc, arrays):
    io = {n: nc.dram_tensor(f"in_{n}", a.shape, mybir.dt.from_np(a.dtype), kind="ExternalInput").ap()
          for n, a in arrays.items()}
    io["out"] = nc.dram_tensor("out_0", (B, T, C), F32, kind="ExternalOutput").ap()
    hybrid_kernel(nc, io)


def kernel(**inputs):
    import concourse.bacc as _bacc
    from concourse.bass_utils import run_bass_kernel_spmd as _run

    arrays = device_inputs(inputs)
    nc = _bacc.Bacc("TRN2", target_bir_lowering=False, num_devices=1)
    program(nc, arrays)
    r = _run(nc, [{f"in_{n}": a for n, a in arrays.items()}], core_ids=[0])
    return r.results[0]["out_0"]
```
